# Optimizing a Trainium2 kernel written in Bass

```python
import numpy as np
import jax
import jax.numpy as jnp

def _softmax(x, axis=-1):
    return jax.nn.softmax(x, axis=axis)

def _gelu(x):
    return jax.nn.gelu(x, approximate=True)

def _silu(x):
    return jax.nn.silu(x)

def _sigmoid(x):
    return jax.nn.sigmoid(x)

def _layernorm(x, axis=-1, eps=1e-05):
    m = jnp.mean(x, axis=axis, keepdims=True)
    v = jnp.var(x, axis=axis, keepdims=True)
    return (x - m) / jnp.sqrt(v + eps)

def _scatter_add(tgt, idx, src, axis=0):
    return tgt.at[idx].add(src)

def _segment_sum(src, seg, n):
    return jax.ops.segment_sum(src, seg, n)
kernel_name = 'mk_gnn_resnorm_d4_gnn_r32_b06975'

def setup_inputs(seed: int=0):
    np.random.seed(seed)
    _w = jnp.asarray

    def _rec_inputs():
        import jax
        import jax.numpy as jnp
        _gk = jax.random.key(seed)
        x = -0.0006008 + 1.001 * jax.random.normal(jax.random.fold_in(_gk, 1), (3125, 128), jnp.float32)
        src = jax.random.randint(jax.random.fold_in(_gk, 2), (100000,), 0, 3125, jnp.int32)
        dst = jnp.minimum((3125 * jax.random.uniform(jax.random.fold_in(_gk, 3), (100000,)) ** 2.0).astype(jnp.int32), 99999)
        _o = jnp.argsort(dst, stable=True)
        src = src[_o]
        dst = dst[_o]
        edge_attr_16 = 0.000268479 + 0.999861 * jax.random.normal(jax.random.fold_in(_gk, 11), (100000, 16), jnp.float32)
        edge_attr_6 = 0.00011001 + 1.00018 * jax.random.normal(jax.random.fold_in(_gk, 12), (100000, 6), jnp.float32)
        return (x, src, dst, edge_attr_16, edge_attr_6)
    x, src, dst, edge_attr_16, edge_attr_6 = _rec_inputs()

    def _L0_gnn_setup():
        import jax, jax.numpy as jnp
        import numpy as np
        HEADS = 4
        OUT_F = 32
        EDGE_F = 16
        ALPHA = 0.2
        key = jax.random.key(seed)
        k1, k2, k3, k4, k5 = jax.random.split(key, 5)
        N, E, IN_F = (625, 20000, 128)
        h = jax.random.normal(k1, (N, IN_F), dtype=jnp.float32)
        edge_index = jax.random.randint(k2, (2, E), 0, N, dtype=jnp.int64)
        edge_attr = jax.random.normal(k3, (E, EDGE_F), dtype=jnp.float32)
        W = jax.random.normal(k4, (IN_F, HEADS * OUT_F), dtype=jnp.float32) * 0.1
        a = jax.random.normal(k5, (HEADS, 2 * OUT_F + EDGE_F), dtype=jnp.float32) * 0.1
        return {'h': h, 'edge_index': edge_index, 'edge_attr': edge_attr, 'W': W, 'a': a}
    _L0_gnn_all = _L0_gnn_setup()
    _L0_gnn_in = {k: v for k, v in _L0_gnn_all.items() if k in ('W', 'a')}
    del _L0_gnn_all

    def _L1_gnn_setup():
        import jax, jax.numpy as jnp
        import numpy as np
        NUM_NODES = 3125
        NUM_EDGES = 50000
        IN_DIM = 128
        OUT_DIM = 128
        key = jax.random.key(seed)
        k_x, k_e, k_wn, k_bn, k_ws, k_bs = jax.random.split(key, 6)
        x = jax.random.normal(k_x, (NUM_NODES, IN_DIM), dtype=jnp.float32)
        edge_index = jax.random.randint(k_e, (2, NUM_EDGES), 0, NUM_NODES, dtype=jnp.int64)
        s = 1.0 / np.sqrt(IN_DIM)
        W_neigh = jax.random.uniform(k_wn, (OUT_DIM, IN_DIM), dtype=jnp.float32, minval=-s, maxval=s)
        b_neigh = jax.random.uniform(k_bn, (OUT_DIM,), dtype=jnp.float32, minval=-s, maxval=s)
        W_self = jax.random.uniform(k_ws, (OUT_DIM, IN_DIM), dtype=jnp.float32, minval=-s, maxval=s)
        b_self = jax.random.uniform(k_bs, (OUT_DIM,), dtype=jnp.float32, minval=-s, maxval=s)
        return {'x': x, 'edge_index': edge_index, 'W_neigh': W_neigh, 'b_neigh': b_neigh, 'W_self': W_self, 'b_self': b_self}
    _L1_gnn_all = _L1_gnn_setup()
    _L1_gnn_in = {k: v for k, v in _L1_gnn_all.items() if k in ('W_neigh', 'b_neigh', 'W_self', 'b_self')}
    del _L1_gnn_all

    def _L2_gnn_setup():
        import jax, jax.numpy as jnp
        import numpy as np
        N, E, D, H = (3125, 18750, 128, 512)
        key = jax.random.key(seed)
        ks = jax.random.split(key, 9)
        s = 0.05
        return {'z': jax.random.normal(ks[0], (N, D), dtype=jnp.float32), 'edge_index': jax.random.randint(ks[1], (2, E), 0, N, dtype=jnp.int64), 'Wg': jax.random.normal(ks[2], (D, D), dtype=jnp.float32) * s, 'Ws': jax.random.normal(ks[3], (D, D), dtype=jnp.float32) * s, 'bg': jnp.zeros((D,), dtype=jnp.float32), 'W1': jax.random.normal(ks[4], (D, H), dtype=jnp.float32) * s, 'b1': jnp.zeros((H,), dtype=jnp.float32), 'W2': jax.random.normal(ks[5], (H, H), dtype=jnp.float32) * s, 'b2': jnp.zeros((H,), dtype=jnp.float32), 'W3': jax.random.normal(ks[6], (H, D), dtype=jnp.float32) * s, 'b3': jnp.zeros((D,), dtype=jnp.float32)}
    _L2_gnn_all = _L2_gnn_setup()
    _L2_gnn_in = {k: v for k, v in _L2_gnn_all.items() if k in ('Wg', 'Ws', 'bg', 'W1', 'b1', 'W2', 'b2', 'W3', 'b3')}
    del _L2_gnn_all

    def _L3_gnn_setup():
        import jax, jax.numpy as jnp
        import numpy as np
        N_NODES = 50000
        N_EDGES = 25000
        IN_F = 128
        OUT_F = 128
        EDGE_F = 6
        key = jax.random.key(seed)
        k1, k2, k3, k4, k5, k6, k7 = jax.random.split(key, 7)
        nodeFeatures = jax.random.normal(k1, (N_NODES, IN_F), dtype=jnp.float32)
        edgeIndex = jax.random.randint(k2, (N_EDGES, 2), 0, N_NODES, dtype=jnp.int64)
        edgeFeatures = jax.random.normal(k3, (N_EDGES, EDGE_F), dtype=jnp.float32)
        lim_n = 1.0 / np.sqrt(IN_F)
        lim_e = 1.0 / np.sqrt(EDGE_F)
        W = jax.random.uniform(k4, (IN_F, OUT_F), minval=-lim_n, maxval=lim_n, dtype=jnp.float32)
        b = jax.random.uniform(k5, (OUT_F,), minval=-lim_n, maxval=lim_n, dtype=jnp.float32)
        We = jax.random.uniform(k6, (EDGE_F, OUT_F), minval=-lim_e, maxval=lim_e, dtype=jnp.float32)
        be = jax.random.uniform(k7, (OUT_F,), minval=-lim_e, maxval=lim_e, dtype=jnp.float32)
        return {'nodeFeatures': nodeFeatures, 'edgeIndex': edgeIndex, 'edgeFeatures': edgeFeatures, 'W': W, 'b': b, 'We': We, 'be': be}
    _L3_gnn_all = _L3_gnn_setup()
    _L3_gnn_in = {k: v for k, v in _L3_gnn_all.items() if k in ('W', 'b', 'We', 'be')}
    del _L3_gnn_all
    return {'x': x, 'src': src, 'dst': dst, 'edge_attr_16': edge_attr_16, 'edge_attr_6': edge_attr_6, 'L0_gnn_W': _L0_gnn_in['W'], 'L0_gnn_a': _L0_gnn_in['a'], 'L1_gnn_W_neigh': _L1_gnn_in['W_neigh'], 'L1_gnn_b_neigh': _L1_gnn_in['b_neigh'], 'L1_gnn_W_self': _L1_gnn_in['W_self'], 'L1_gnn_b_self': _L1_gnn_in['b_self'], 'L2_gnn_Wg': _L2_gnn_in['Wg'], 'L2_gnn_Ws': _L2_gnn_in['Ws'], 'L2_gnn_bg': _L2_gnn_in['bg'], 'L2_gnn_W1': _L2_gnn_in['W1'], 'L2_gnn_b1': _L2_gnn_in['b1'], 'L2_gnn_W2': _L2_gnn_in['W2'], 'L2_gnn_b2': _L2_gnn_in['b2'], 'L2_gnn_W3': _L2_gnn_in['W3'], 'L2_gnn_b3': _L2_gnn_in['b3'], 'L3_gnn_W': _L3_gnn_in['W'], 'L3_gnn_b': _L3_gnn_in['b'], 'L3_gnn_We': _L3_gnn_in['We'], 'L3_gnn_be': _L3_gnn_in['be']}

def reference(x, src, dst, edge_attr_16, edge_attr_6, L0_gnn_W, L0_gnn_a, L1_gnn_W_neigh, L1_gnn_b_neigh, L1_gnn_W_self, L1_gnn_b_self, L2_gnn_Wg, L2_gnn_Ws, L2_gnn_bg, L2_gnn_W1, L2_gnn_b1, L2_gnn_W2, L2_gnn_b2, L2_gnn_W3, L2_gnn_b3, L3_gnn_W, L3_gnn_b, L3_gnn_We, L3_gnn_be):
    import jax
    import jax.numpy as jnp

    def _L0_gnn_ref(h, edge_index, edge_attr, W, a):
        import jax, jax.numpy as jnp
        import numpy as np
        HEADS = 4
        OUT_F = 32
        EDGE_F = 16
        ALPHA = 0.2
        N = h.shape[0]
        Wh = (h @ W).reshape(N, HEADS, OUT_F)
        src = edge_index[0]
        dst = edge_index[1]
        a_src = a[:, :OUT_F]
        a_dst = a[:, OUT_F:2 * OUT_F]
        a_edge = a[:, 2 * OUT_F:]
        e = jnp.einsum('ehd,hd->eh', Wh[src], a_src) + jnp.einsum('ehd,hd->eh', Wh[dst], a_dst) + edge_attr @ a_edge.T
        e = jnp.where(e >= 0, e, ALPHA * e)
        attention = jax.nn.softmax(e, axis=1)
        msg = attention[:, :, None] * Wh[dst]
        h_prime = jnp.zeros_like(Wh).at[src].add(msg)
        out = h_prime.reshape(N, HEADS * OUT_F)
        return jax.nn.elu(out)

    def _L1_gnn_ref(x, edge_index, W_neigh, b_neigh, W_self, b_self):
        import jax, jax.numpy as jnp
        import numpy as np
        NUM_NODES = 3125
        NUM_EDGES = 50000
        IN_DIM = 128
        OUT_DIM = 128
        src, dst = (edge_index[0], edge_index[1])
        msgs = x[src]
        neigh = jax.ops.segment_sum(msgs, dst, num_segments=x.shape[0])
        neigh_proj = neigh @ W_neigh.T + b_neigh
        self_proj = x @ W_self.T + b_self
        return neigh_proj + self_proj

    def _L2_gnn_ref(z, edge_index, Wg, Ws, bg, W1, b1, W2, b2, W3, b3):
        import jax, jax.numpy as jnp
        import numpy as np
        N, E, D, H = (3125, 18750, 128, 512)
        src, dst = (edge_index[0], edge_index[1])
        n = z.shape[0]
        msgs = z[src]
        agg = jax.ops.segment_sum(msgs, dst, num_segments=n)
        deg = jax.ops.segment_sum(jnp.ones((src.shape[0],), z.dtype), dst, num_segments=n)
        agg = agg / jnp.maximum(deg, 1.0)[:, None]
        h = jax.nn.relu(agg @ Wg + z @ Ws + bg)
        h = jnp.tanh(h @ W1 + b1)
        h = jnp.tanh(h @ W2 + b2)
        return h @ W3 + b3

    def _L3_gnn_ref(nodeFeatures, edgeIndex, edgeFeatures, W, b, We, be):
        import jax, jax.numpy as jnp
        import numpy as np
        N_NODES = 50000
        N_EDGES = 25000
        IN_F = 128
        OUT_F = 128
        EDGE_F = 6
        transformed = nodeFeatures @ W + b
        edgeMsg = edgeFeatures @ We + be
        src = edgeIndex[:, 0]
        dst = edgeIndex[:, 1]
        messages = transformed[src] + edgeMsg
        aggregated = jax.ops.segment_sum(messages, dst, num_segments=nodeFeatures.shape[0])
        return jax.nn.relu(aggregated)
    edge_index = jnp.stack([src, dst])
    edge_index_t = jnp.stack([src, dst], axis=1)
    x = _layernorm(x + _L0_gnn_ref(x, edge_index, edge_attr_16, L0_gnn_W, L0_gnn_a), axis=-1)
    x = _layernorm(x + _L1_gnn_ref(x, edge_index, L1_gnn_W_neigh, L1_gnn_b_neigh, L1_gnn_W_self, L1_gnn_b_self), axis=-1)
    x = _layernorm(x + _L2_gnn_ref(x, edge_index, L2_gnn_Wg, L2_gnn_Ws, L2_gnn_bg, L2_gnn_W1, L2_gnn_b1, L2_gnn_W2, L2_gnn_b2, L2_gnn_W3, L2_gnn_b3), axis=-1)
    x = _layernorm(x + _L3_gnn_ref(x, edge_index_t, edge_attr_6, L3_gnn_W, L3_gnn_b, L3_gnn_We, L3_gnn_be), axis=-1)
    return x

_drawn_inputs = setup_inputs


def setup_inputs(seed=0):
    import zlib

    import numpy as np

    out = dict(_drawn_inputs(seed))
    spreads = {'L2_gnn_bg': (0.0, 0.1),
     'L2_gnn_b1': (0.0, 0.1),
     'L2_gnn_b2': (0.0, 0.1),
     'L2_gnn_b3': (0.0, 0.1)}
    factors = {'L1_gnn_b_neigh': 5.051, 'L1_gnn_b_self': 3.672}
    for name, (base, spread) in spreads.items():
        noise = np.random.default_rng([zlib.crc32(name.encode()), seed]).standard_normal(out[name].shape)
        drawn = base * np.exp(spread * noise) if base else spread * noise
        out[name] = jnp.asarray(drawn.astype(out[name].dtype))
    for name, factor in factors.items():
        out[name] = (out[name] * factor).astype(out[name].dtype)
    return out
```

```python
import concourse.bass as bass
from concourse import mybir
from contextlib import ExitStack

FP32 = mybir.dt.float32
BF16 = mybir.dt.bfloat16
FP16 = mybir.dt.float16
I32 = mybir.dt.int32
ALU = mybir.AluOpType
ACT = mybir.ActivationFunctionType
AX = mybir.AxisListType.X
ds = bass.ds

N = 3125
E = 100000
F = 128
HEADS, HF = 4, 32
EF0, EF3 = 16, 6
HID = 512
KH = HID // F

TS = 96
NT = -(-N // TS)
LAST = N - TS * (NT - 1)
NPAD = NT * TS
EP, EC = 125, 800
CH = 128
GR = 4
UN = 4
NC = -(-(E // CH + NT) // (GR * UN)) * GR * UN
NG = NC // GR
SLOTS = GR * UN
BANK = 512
DW = 3136
DB = [(b * BANK, min(BANK, DW - b * BANK)) for b in range(-(-DW // BANK))]
CEN = 1562
W = 16
R_DST, R_DC, R_SL, R_EA, R_E6 = 0, 1, 2, 3, 7
TW = F + HEADS
E6C = 3 * EF3
OCOL = TS + E6C
HCOL = 64
FAR = 20000.0
XS = 4096.0
ALPHA = 0.2
EPS = 1e-5
RNE = 12582912.0
AR = 4
BT = 4
NB = -(-NT // BT)


class Steps:

    def __init__(self, eng, sem):
        self.eng, self.sem, self.n, self.at = eng, sem, 0, 0

    def done(self, ins):
        ins.then_inc(self.sem, 1)
        self.n += 1

    def wait(self):
        self.eng.wait_ge(self.sem, self.at + self.n)

    def __call__(self, ins):
        self.done(ins)
        self.wait()


def gnn_stack(nc, x, src, dst, ea16, ea6, W0, a0, Wn, bn, Wsf, bs, Wg, Ws, bg, W1, b1, W2, b2, W3, b3, W4, b4, We, be, out):
    ctx = ExitStack()
    with ctx:
        def sb(name, shape, dt=FP32):
            return ctx.enter_context(nc.sbuf_tensor(name, shape, dt))

        def sem(name):
            return ctx.enter_context(nc.semaphore(name))

        def dram(name, shape, dt=FP32):
            return nc.dram_tensor(name, shape, dt, kind="Internal").ap()

        table = dram("table", [NPAD, TW])
        records = dram("records", [CH * NC, W])
        counts = dram("counts", [NT, TS, DW], FP16)

        arenaA = sb("arenaA", [128, NC * W])
        arenaB = sb("arenaB", [128, EC * W])
        arenaC = sb("arenaC", [128, 6 * EC + 500])
        ident = sb("ident", [128, 128])
        identb = sb("identb", [128, 128], BF16)
        ones = sb("ones", [128, 128])
        zerob = sb("zerob", [128, 128], BF16)
        tril = sb("tril", [128, 128])
        degsel = sb("degsel", [128, F])
        iotad = sb("iotad", [128, DW], FP16)
        iotas = sb("iotas", [128, TS], BF16)
        binid = sb("binid", [128, NT])
        xs = sb("xs", [128, NT, F])
        ys = sb("ys", [128, NT, F])
        xT = sb("xT", [F, NPAD])
        esum = sb("esum", [128, NPAD])
        w0s = sb("w0s", [F, F])
        w0T = sb("w0T", [F, F])
        ablk = sb("ablk", [F, 2 * HEADS])
        edgeblk = sb("edgeblk", [128, 8 * HEADS])
        wcat = sb("wcat", [F, F + 2 * HEADS])
        wnT = sb("wnT", [F, F])
        wsT = sb("wsT", [F, F])
        wgs = sb("wgs", [F, 2, F])
        w4s = sb("w4s", [F, F])
        wext = sb("wext", [128, F])
        brow1 = sb("brow1", [2, F])
        brow3 = sb("brow3", [1, F])
        bcol = sb("bcol", [F, 1 + 2 * KH])
        ssrc = sb("ssrc", [TS, NT, HEADS])
        s3 = sb("s3", [TS, NT, HEADS, 3], BF16)
        bins = sb("bins", [128, 8, NT])
        binsi = sb("binsi", [128, NT], I32)
        tmap = sb("tmap", [1, 2, NC + 1], I32)
        st = sb("st", [128, 3, NT])
        places = sb("places", [EP, 2, SLOTS], I32)
        rowid = sb("rowid", [128, SLOTS], I32)
        zerow = sb("zerow", [128, BANK])
        smalls = sb("smalls", [128, 2, 48])

        ea16s = arenaA[0:EP, 0:EC * EF0]
        rec = arenaB[0:EP, :].rearrange("p (c w) -> p c w", w=W)
        recb = arenaB[0:EP, :].bitcast(BF16).rearrange("p (c w) -> p c w", w=2 * W)
        parts = [arenaC[0:EP, k * EC:(k + 1) * EC] for k in range(6)]
        srci, dsti = parts[0].bitcast(I32), parts[1].bitcast(I32)
        mask, cum, srcf, tidf, pos, zero = parts
        posi, parti = parts[5].bitcast(I32), parts[1].bitcast(I32)
        eT = arenaC[:, 6 * EC:6 * EC + 4 * EP]
        ein = xT[0:EP, 0:512]
        batch = xT[0:EP, 512:512 + 2 * SLOTS * W].rearrange("p (h s w) -> p h s w", h=2, s=SLOTS)
        HE = EC // 2 * EF3
        ysflat = ys[:, :, :].rearrange("p t f -> p (t f)")
        e6h = [ysflat[0:EP, 0:HE], esum[0:EP, 0:HE]]
        TP = 3
        TT = NT // TP
        tpiece = ysflat[0:TS, HE:HE + TT * TW].rearrange("p (t w) -> p t w", w=TW)
        SP_ = 24
        sent = esum[:, HE:HE + NC // SP_ * W].rearrange("p (c w) -> p c w", w=W)
        mf = arenaC[0:1, 0:2 * (NC + 1)].rearrange("p (k c) -> p k c", k=2)
        recs = arenaA[:, :].rearrange("p (c w) -> p c w", w=W)
        recsb = arenaA[:, :].bitcast(BF16).rearrange("p (c w) -> p c w", w=2 * W)
        hot = [arenaB[:, s * DW // 2:(s + 1) * DW // 2].bitcast(FP16) for s in range(GR)]
        o = GR * DW // 2
        stage = arenaB[0:TS, o:o + DW].bitcast(FP16); o += DW
        msg = arenaB[:, o:o + 2 * GR * F].rearrange("p (s f) -> p s f", f=F); o += 2 * GR * F
        gt = arenaB[:, o:o + SLOTS * TW].rearrange("p (s w) -> p s w", w=TW); o += SLOTS * TW
        assert o <= EC * W
        o = 0
        stat = arenaC[:, o:o + UN * GR * 64].bitcast(BF16).rearrange("p (s f) -> p s f", f=128); o += UN * GR * 64
        statf = arenaC[:, o:o + UN * GR * TS].rearrange("p (s f) -> p s f", f=TS); o += UN * GR * TS
        dT = arenaC[0:TS, o:o + UN * GR * 64].bitcast(BF16).rearrange("p (s f) -> p s f", f=128); o += UN * GR * 64
        assert o <= 6 * EC
        ring = arenaB[0:TS, 0:AR * DW // 2].bitcast(FP16).rearrange("p (s d) -> p s d", s=AR)
        o = (AR + 1) * DW // 2
        ring0 = arenaB[0:TS, AR * DW // 2:o].bitcast(FP16)
        w1s = arenaB[:, o:o + HID]; o += HID
        w2s = arenaB[:, o:o + KH * HID].rearrange("p (k n) -> p k n", k=KH); o += KH * HID
        w3s = arenaB[:, o:o + KH * F].rearrange("p (k n) -> p k n", k=KH); o += KH * F
        assert o <= EC * W
        scr = arenaA[0:TS, 0:NT * F].rearrange("p (t f) -> p t f", f=F)
        xh = arenaA[0:TS, 0:NT * F // 2].bitcast(FP16).rearrange("p (t f) -> p t f", f=F)
        xl = arenaA[0:TS, NT * F // 2:NT * F].bitcast(FP16).rearrange("p (t f) -> p t f", f=F)
        neT = arenaA[:, NT * F:NT * F + NPAD]
        rdeg = arenaA[:, NT * F + NPAD:NT * F + 2 * NPAD]
        assert NT * F + 2 * NPAD <= NC * W
        BW = BT * TS
        h0 = arenaC[:, 0:BW]
        h1 = arenaC[:, BW:BW * (1 + KH)].rearrange("p (k n) -> p k n", k=KH)
        h2 = arenaC[:, BW * (1 + KH):BW * (1 + 2 * KH)].rearrange("p (k n) -> p k n", k=KH)
        xr, yr = xs[0:TS, :, :], ys[0:TS, :, :]

        acc = [ctx.enter_context(nc.psum_tensor(f"acc{b}", [128, BANK], FP32)) for b in range(8)]
        psT = acc[7][0:TS, 0:256].bitcast(BF16).rearrange("p (j e) -> p j e", j=GR)
        psS = acc[7][:, 256:256 + GR * HEADS * 3]

        ld_ends, ld_x, ld_e16, ld_e6, ld_w, ld_w2, ld_w3 = (
            sem(n) for n in ("ld_ends", "ld_x", "ld_e16", "ld_e6", "ld_w", "ld_w2", "ld_w3"))
        pool_step, pool_passed, consts, sent_done, e6_split = (sem(n) for n in ("pool_step", "pool_passed", "consts", "sent_done", "e6_split"))
        prep_in, prep_out = sem("prep_in"), sem("prep_out")
        piece_ready, piece_done = sem("piece_ready"), sem("piece_done")
        ein_ready, eT_in, eT_out, el_in, el_out = (sem(n) for n in ("ein_ready", "eT_in", "eT_out", "el_in", "el_out"))
        dve_step, act_step = sem("dve_step"), sem("act_step")
        totals_ready, prefix_in, rank_done = (sem(n) for n in ("totals_ready", "prefix_in", "rank_done"))
        maps_ready, recs_in = sem("maps_ready"), sem("recs_in")
        scattered = [sem(f"scattered{h}") for h in range(2)]
        gathered = [sem(f"gathered{s}") for s in range(SLOTS)]
        stat_ready, statf_ready, turned, dT_ready = (sem(n) for n in ("stat_ready", "statf_ready", "turned", "dT_ready"))
        src_logits, looked, shifted, exped, msg_ready = (sem(n) for n in ("src_logits", "looked", "shifted", "exped", "msg_ready"))
        hot_ready, main_done, evac_done, stage_free, stored = (
            sem(n) for n in ("hot_ready", "main_done", "evac_done", "stage_free", "stored"))
        offs_read, zero_ready, chunk_ids, esum_ready = (sem(n) for n in ("offs_read", "zero_ready", "chunk_ids", "esum_ready"))
        count_in = [sem(f"count_in{s}") for s in range(AR + 1)]
        elu_in, elu_exp, root_in, root_out, x_ready = (sem(n) for n in ("elu_in", "elu_exp", "root_in", "root_out", "x_ready"))
        xh_ready, halves_ready, xT_in, xT_ready = (sem(n) for n in ("xh_ready", "halves_ready", "xT_in", "xT_ready"))
        tile_used, neigh_out, deg_in, deg_out = (sem(n) for n in ("tile_used", "neigh_out", "deg_in", "deg_out"))
        blk_ready, blk_used, out_done = sem("blk_ready"), sem("blk_used"), sem("out_done")
        mlp_in, mlp_out = sem("mlp_in"), sem("mlp_out")

        TURNS = NG // UN
        block = ctx.enter_context(nc.Block())

        @block.sync
        def _(sp):
            for lo, hi in ((0, 112), (112, EP)):
                sp.dma_start(srci[lo:hi, :], src.rearrange("(p c) -> p c", p=EP)[lo:hi, :]).then_inc(ld_ends, 16)
                sp.dma_start(dsti[lo:hi, :], dst.rearrange("(p c) -> p c", p=EP)[lo:hi, :]).then_inc(ld_ends, 16)
            sp.wait_ge(consts, 1)
            sp.dma_start(xs[0:TS, 0:NT - 1, :], x[0:TS * (NT - 1), :].rearrange("(t p) f -> p t f", p=TS)).then_inc(ld_x, 16)
            sp.dma_start(xs[0:LAST, NT - 1, :], x[TS * (NT - 1):N, :]).then_inc(ld_x, 16)
            sp.dma_start(w0s[:, :], W0).then_inc(ld_w, 16)
            for h in range(HEADS):
                for k in range(2):
                    sp.dma_start(ablk[HF * h:HF * h + HF, HEADS * (1 - k) + h:HEADS * (1 - k) + h + 1],
                                 a0[h:h + 1, HF * k:HF * k + HF].rearrange("a d -> d a"), allow_slow_non_contiguous=True).then_inc(ld_w, 16)
            for j in range(8):
                sp.dma_start(edgeblk[EF0 * j:EF0 * j + EF0, HEADS * j:HEADS * j + HEADS],
                             a0[:, 2 * HF:2 * HF + EF0].rearrange("h d -> d h"), allow_slow_non_contiguous=True).then_inc(ld_w, 16)
            for lo, hi in ((0, 112), (112, EP)):
                sp.dma_start(ea16s[lo:hi, :], ea16.rearrange("(p c) d -> p (c d)", p=EP)[lo:hi, :]).then_inc(ld_e16, 16)
                for k in range(2):
                    sp.dma_start(e6h[k][lo:hi, :],
                                 ea6.rearrange("(p c) d -> p (c d)", p=EP)[lo:hi, k * HE:(k + 1) * HE]).then_inc(ld_e6, 16)
            for k in range(SP_):
                sp.dma_start(records.rearrange("(p c) w -> p c w", c=NC)[:, k * (NC // SP_):(k + 1) * (NC // SP_), :],
                             sent).then_inc(sent_done, 16)
            for to, frm in ((wnT[:, :], Wn), (wsT[:, :], Wsf),
                            (wgs[:, 0, :], Wg), (wgs[:, 1, :], Ws), (w4s[:, :], W4),
                            (brow1[0:1, :], bn.rearrange("(a f) -> a f", a=1)),
                            (brow1[1:2, :], bs.rearrange("(a f) -> a f", a=1)),
                            (brow3[0:1, :], b3.rearrange("(a f) -> a f", a=1)),
                            (bcol[:, 0:1], bg.rearrange("(p a) -> p a", a=1)),
                            (bcol[:, 1:1 + KH], b1.rearrange("(k p) -> p k", p=F)),
                            (bcol[:, 1 + KH:1 + 2 * KH], b2.rearrange("(k p) -> p k", p=F)),
                            (wext[TS:TS + EF3, :], We), (wext[TS + EF3:TS + 2 * EF3, :], We),
                            (wext[TS + 2 * EF3:OCOL, :], We),
                            (wext[OCOL:OCOL + 1, :], b4.rearrange("(a f) -> a f", a=1)),
                            (wext[OCOL + 1:OCOL + 2, :], be.rearrange("(a f) -> a f", a=1))):
                sp.dma_start(to, frm, allow_slow_non_contiguous=True).then_inc(ld_w2, 16)
            for k in range(TP):
                sp.wait_ge(piece_ready, k + 1)
                sp.dma_start(table[k * TT * TS:(k + 1) * TT * TS, :].rearrange("(t p) f -> p t f", p=TS),
                             tpiece).then_inc(piece_done, 16)
            for h in range(2):
                sp.wait_ge(scattered[h], 8 * EC)
            sp.dma_start(arenaA[:, :], records.rearrange("(p c) w -> p (c w)", c=NC)).then_inc(recs_in, 16)
            sp.sem_inc(stage_free, 2)
            with sp.Fori(0, NT) as t:
                sp.wait_ge(evac_done, t + 2)
                sp.dma_start(counts[ds(t, 1), :, :].rearrange("t p d -> p (t d)"),
                             stage[:, ds((t % 2) * DW, DW)]).then_inc(stored, 16)
                sp.wait_ge(stored, t * 16 + 16)
                sp.sem_inc(stage_free, 1)
            sp.wait_ge(main_done, NC)
            sp.wait_ge(msg_ready, NG)
            for to, frm in ((w1s, W1), (w2s, W2.rearrange("(k p) n -> p k n", p=F)), (w3s, W3.rearrange("(k p) n -> p k n", p=F))):
                sp.dma_start(to, frm).then_inc(ld_w3, 16)
            for lay in range(3):
                if lay:
                    sp.wait_ge(tile_used, NT * lay)
                sp.dma_start(ring0, counts[0, :, :]).then_inc(count_in[AR], 16)
                for s in range(AR):
                    sp.dma_start(ring[:, s, :], counts[1 + s, :, :]).then_inc(count_in[s], 16)
                with sp.Fori(1, (NT - 1) // AR) as i:
                    for s in range(AR):
                        sp.wait_ge(tile_used, i * AR + (NT * lay + 2 + s - AR))
                        sp.dma_start(ring[:, s, :],
                                     counts[ds(i * AR + (1 + s), 1), :, :].rearrange("t p d -> p (t d)")).then_inc(count_in[s], 16)
            sp.wait_ge(x_ready, 4)
            sp.dma_start(out[0:TS * (NT - 1), :].rearrange("(t p) f -> p t f", p=TS), xs[0:TS, 0:NT - 1, :]).then_inc(out_done, 16)
            sp.dma_start(out[TS * (NT - 1):N, :], xs[0:LAST, NT - 1, :]).then_inc(out_done, 16)
            sp.wait_ge(out_done, 32)

        @block.gpsimd
        def _(pool):
            step = Steps(pool, pool_step)
            step.done(nc.gpsimd.memset(xs[:, NT - 1, :], 0.0))
            step.done(nc.gpsimd.memset(ablk[:, :], 0.0))
            step.done(nc.gpsimd.memset(wext[:, :], 0.0))
            step.done(nc.gpsimd.memset(sent[:, :, :], 0.0))
            step(nc.gpsimd.memset(edgeblk[:, :], 0.0))
            step(nc.gpsimd.memset(sent[:, :, R_DC:R_SL + 1], FAR))
            nc.gpsimd.memset(zerob[:, :], 0.0).then_inc(consts, 1)
            step.done(nc.gpsimd.memset(ones[:, :], 1.0))
            step.done(nc.gpsimd.memset(ident[:, :], 0.0))
            step.done(nc.gpsimd.memset(degsel[:, :], 0.0))
            step(nc.gpsimd.memset(tril[:, :], 1.0))
            step.done(nc.gpsimd.affine_select(out=tril[:, :], in_=tril[:, :], compare_op=ALU.is_gt, fill=0.0,
                                              base=0, pattern=[[1, 128]], channel_multiplier=-1))
            step.done(nc.gpsimd.affine_select(out=degsel[:, :], in_=degsel[:, :], compare_op=ALU.not_equal, fill=1.0,
                                              base=-OCOL, pattern=[[0, F]], channel_multiplier=1))
            step.done(nc.gpsimd.iota(binid[:, :], pattern=[[1, NT]], base=0, channel_multiplier=0,
                                     allow_small_or_imprecise_dtypes=True))
            step(nc.gpsimd.affine_select(out=ident[:, :], in_=ident[:, :], compare_op=ALU.not_equal, fill=1.0,
                                         base=0, pattern=[[-1, 128]], channel_multiplier=1))
            nc.gpsimd.tensor_copy(identb[:, :], ident[:, :]).then_inc(consts, 1)
            step.done(nc.gpsimd.iota(iotad[:, :], pattern=[[1, DW]], base=-CEN, channel_multiplier=0,
                                     allow_small_or_imprecise_dtypes=True))
            step(nc.gpsimd.iota(iotas[:, :], pattern=[[1, TS]], base=0, channel_multiplier=0,
                                     allow_small_or_imprecise_dtypes=True))
            pool.sem_inc(consts, 1)
            pool.wait_ge(ld_e6, 64)
            for k in range(2):
                e = e6h[k].rearrange("p (c d) -> p c d", d=EF3)
                to = recb[:, k * (EC // 2):(k + 1) * (EC // 2), :]
                for part in range(3):
                    at = 2 * R_E6 + EF3 * part
                    step(nc.gpsimd.tensor_copy(to[:, :, at:at + EF3], e))
                    if part < 2:
                        step(nc.gpsimd.tensor_tensor(e, e, to[:, :, at:at + EF3], ALU.subtract))
            pool.wait_ge(sent_done, 16 * SP_)
            pool.wait_ge(rank_done, 1)
            nc.gpsimd.iota(mf[:, 1, :], pattern=[[1, NC + 1]], base=0, channel_multiplier=0,
                           allow_small_or_imprecise_dtypes=True).then_inc(chunk_ids, 1)
            pool.wait_ge(el_out, EC // 32)
            HALF = SLOTS

            def scatter(i):
                for h in range(2):
                    c0 = i * (2 * HALF) + h * HALF
                    if not isinstance(i, int):
                        pool.wait_ge(scattered[h], i * (16 * HALF))
                    step.done(nc.gpsimd.tensor_copy(places[:, h, :], posi[:, ds(c0, HALF)]))
                    step(nc.gpsimd.tensor_copy(batch[:, h, :, :], rec[:, ds(c0, HALF), :]))
                    pool.sem_inc(pool_passed, 1)
                    for s in range(HALF):
                        nc.gpsimd.indirect_dma_start(
                            out=records, out_offset=bass.IndirectOffsetOnAxis(ap=places[:, h, s:s + 1], axis=0),
                            in_=batch[:, h, s, :], in_offset=None).then_inc(scattered[h], 16)
            scatter(0)
            with pool.Fori(1, EC // (2 * HALF)) as i:
                step.at = i * 4 - 4
                scatter(i)
            step.n += 2 * (EC // HALF) - 8
            step.at = 0
            pool.wait_ge(recs_in, 16)
            pool.wait_ge(piece_done, 16 * TP)

            def gather(i, k):
                c0 = i * SLOTS + k * GR
                step(nc.gpsimd.tensor_copy(
                    rowid[:, k * GR:(k + 1) * GR],
                    recs[:, ds(c0, GR), R_DST:R_DST + 1].rearrange("p c w -> p (c w)").bitcast(I32)))
                pool.sem_inc(pool_passed, 1)
                for s in range(k * GR, (k + 1) * GR):
                    nc.gpsimd.indirect_dma_start(
                        out=gt[:, s, :], out_offset=None, in_=table,
                        in_offset=bass.IndirectOffsetOnAxis(ap=rowid[:, s:s + 1], axis=0)).then_inc(gathered[s], 16)

            for k in range(UN):
                gather(0, k)
            with pool.Fori(1, TURNS) as i:
                step.at = i * UN - UN
                for k in range(UN):
                    pool.wait_ge(msg_ready, i * UN + (k + 1 - UN))
                    gather(i, k)

        @block.tensor
        def _(pe):
            pe.wait_ge(consts, 2)
            pe.wait_ge(ld_w, 16 * (1 + 2 * HEADS + 8))
            nc.tensor.transpose(acc[0][:, 0:F], w0s[:, :], ident[:, :]).then_inc(prep_in, 1)
            pe.wait_ge(prep_out, 1)
            nc.tensor.matmul(acc[1][:, 0:2 * HEADS], w0T[:, :], ablk[:, :], start=True, stop=True).then_inc(prep_in, 1)
            pe.wait_ge(ld_w2, 16 * 16)
            nc.tensor.transpose(acc[2][:, 0:F], wnT[:, :], ident[:, :]).then_inc(prep_in, 1)
            nc.tensor.transpose(acc[3][:, 0:F], wsT[:, :], ident[:, :]).then_inc(prep_in, 1)
            pe.wait_ge(prep_out, 4)
            pe.wait_ge(ld_x, 32)

            def turn_x(q, first):
                if q == 8:
                    pe.wait_ge(xT_ready, first + 1)
                for t in range(q * BT, min(NT, q * BT + BT)):
                    last = nc.tensor.transpose(acc[q % 8][:, (t % BT) * TS:(t % BT + 1) * TS], xs[0:TS, t, :], ident[0:TS, 0:TS])
                last.then_inc(xT_in, 1)

            for q in range(NB):
                turn_x(q, 0)
            pe.wait_ge(xT_ready, NB)
            for t in range(NT):
                if t >= 4:
                    pe.wait_ge(prep_out, 4 + t - 3)
                nc.tensor.matmul(acc[t % 4][0:TS, 0:F + 2 * HEADS], xT[:, t * TS:(t + 1) * TS], wcat[:, :],
                                 start=True, stop=True).then_inc(prep_in, 1)
            pe.wait_ge(totals_ready, 1)
            nc.tensor.matmul(acc[4][0:EP, 0:NT], tril[0:EP, 0:EP], bins[0:EP, 0, :], start=True, stop=True)
            nc.tensor.matmul(acc[4][:, 64:64 + NT], ones[0:EP, :], bins[0:EP, 0, :], start=True, stop=True).then_inc(prefix_in, 1)

            def edge_logits(i):
                pe.wait_ge(ein_ready, i + 1)
                for k in range(4):
                    last = nc.tensor.transpose(acc[5][:, k * EP:(k + 1) * EP], ein[:, k * 128:(k + 1) * 128], ident[0:EP, 0:EP])
                last.then_inc(eT_in, 1)
                pe.wait_ge(eT_out, i + 1)
                for k in range(4):
                    last = nc.tensor.matmul(acc[6][0:EP, k * 32:(k + 1) * 32], eT[:, k * EP:(k + 1) * EP], edgeblk[:, :],
                                            start=True, stop=True)
                last.then_inc(el_in, 1)

            with pe.Fori(0, EC // 32) as i:
                edge_logits(i)

            pe.wait_ge(el_out, EC // 32)
            pe.wait_ge(prep_out, 4 + NT)
            pe.wait_ge(offs_read, 1)
            pe.wait_ge(zero_ready, 1)
            for b in range(7):
                last = nc.tensor.matmul(acc[b][:, :], zerob[:, :], zerow[:, :].bitcast(BF16)[:, 0:BANK], start=True, stop=False, skip_group_check=True)
            pe.wait_ge(maps_ready, 1)

            def turn_stat(i, k):
                pe.wait_ge(stat_ready, i * UN + k + 1)
                if not (isinstance(i, int) and i * UN + k == 0):
                    pe.wait_ge(looked, i * UN + k)
                for j in range(GR):
                    last = nc.tensor.transpose(psT[:, j, :], stat[:, (k % UN) * GR + j, 0:TS], identb[:, :])
                last.then_inc(turned, 1)

            def look_up(i, k):
                pe.wait_ge(dT_ready, i * UN + k + 1)
                for j in range(GR):
                    c = (i * UN + k) * GR + j
                    tile = pe.value_load(tmap[0:1, 1, ds(c, 1)], min_val=0, max_val=NT - 1)
                    last = nc.tensor.matmul(psS[:, j * 12:(j + 1) * 12], dT[:, (k % UN) * GR + j, :],
                                            s3[:, ds(tile, 1), :, :].rearrange("p t h k -> p (t h k)"), start=True, stop=True)
                last.then_inc(src_logits, 1)

            def main(i, k, chunks):
                pe.wait_ge(msg_ready, i * UN + k + 1)
                pe.wait_ge(statf_ready, i * UN + k + 1)
                for j in chunks:
                    c = (i * UN + k) * GR + j
                    s = (k % UN) * GR + j
                    tile = pe.value_load(tmap[0:1, 0, ds(c, 1)], min_val=0, max_val=NT)
                    pe.wait_ge(evac_done, tile + 1)
                    pe.wait_ge(hot_ready, c + 1)
                    for b, (at, n) in enumerate(DB):
                        nc.tensor.matmul(acc[b][:, 0:n], stat[:, s, :], hot[j][:, at:at + n], start=False, stop=False,
                                         skip_group_check=True)
                    nc.tensor.matmul(acc[6][0:TS, HCOL:HCOL + F], statf[:, s, :], msg[:, (k % 2) * GR + j, :],
                                     start=False, stop=False, skip_group_check=True).then_inc(main_done, 1)

            def turn(i, last=False):
                for k in range(UN):
                    main(i, k, (0,))
                    if not (last and k + 2 >= UN):
                        turn_stat(i, k + 2)
                    main(i, k, (1,))
                    if not (last and k + 2 >= UN):
                        look_up(i, k + 2)
                    main(i, k, (2, 3))

            for k in range(2):
                turn_stat(0, k)
                look_up(0, k)
            turn(0)
            with pe.Fori(1, TURNS - 1) as i:
                turn(i)
            turn(TURNS - 1, last=True)

            for lay in range(3):
                pe.wait_ge(x_ready, lay + 1)
                pe.wait_ge(esum_ready, 1)
                if lay:
                    pe.wait_ge(blk_used, NB * lay)
                if lay < 2:
                    for q in range(NB):
                        turn_x(q, NB * (lay + 1))
                    pe.wait_ge(xT_ready, NB * (lay + 2))
                if lay == 0:
                    for b, (at, n) in enumerate(DB):
                        last = nc.tensor.matmul(acc[b][:, 0:n], degsel[TS:128, :], esum[TS:128, at:at + n], start=True, stop=True)
                    last.then_inc(deg_in, 1)
                    pe.wait_ge(deg_out, 1)
                pe.wait_ge(halves_ready, lay + 1)

                def count_tile(k, tile, start):
                    for h, half in enumerate((xh, xl)):
                        for b, (at, n) in enumerate(DB):
                            last = nc.tensor.matmul(acc[b][:, 0:n], half[:, ds(k, 1), :].rearrange("p t f -> p (t f)"),
                                                    tile[:, at:at + n], start=start and h == 0, stop=False,
                                                    skip_group_check=True)
                    last.then_inc(tile_used, 1)

                pe.wait_ge(count_in[AR], 16 * (lay + 1))
                count_tile(0, ring0, True)
                with pe.Fori(0, (NT - 1) // AR) as i:
                    for s in range(AR):
                        pe.wait_ge(count_in[s], i * 16 + 16 * (lay * ((NT - 1) // AR) + 1))
                        count_tile(i * AR + (1 + s), ring[:, s, :], False)
                pe.wait_ge(neigh_out, 7 * (lay + 1))
                for q in range(NB):
                    tiles = range(q * BT, min(NT, q * BT + BT))
                    n = len(tiles) * TS
                    cols = slice(q * BW, q * BW + n)
                    if lay == 1:
                        at = 9 * q
                        nc.tensor.matmul(acc[7][:, 0:n], wgs[:, 0, :], neT[:, cols], start=True, stop=False)
                        nc.tensor.matmul(acc[7][:, 0:n], wgs[:, 1, :], xT[:, cols], start=False, stop=True).then_inc(mlp_in, 1)
                        pe.wait_ge(mlp_out, at + 1)
                        if q == 0:
                            pe.wait_ge(ld_w3, 48)
                        if q:
                            pe.wait_ge(blk_used, NB + q)
                        for m in range(KH):
                            nc.tensor.matmul(acc[m][:, 0:n], w1s[:, m * F:(m + 1) * F], h0[:, 0:n], start=True, stop=True).then_inc(mlp_in, 1)
                        pe.wait_ge(mlp_out, at + 5)
                        for m in range(KH):
                            for k in range(KH):
                                last = nc.tensor.matmul(acc[4 + m][:, 0:n], w2s[:, k, m * F:(m + 1) * F], h1[:, k, 0:n],
                                                        start=k == 0, stop=k == KH - 1)
                            last.then_inc(mlp_in, 1)
                        pe.wait_ge(mlp_out, at + 9)
                        bank = 0
                    else:
                        bank = q % 8
                        if q == 8:
                            pe.wait_ge(blk_used, NB * lay + 1)
                    for j, t in enumerate(tiles):
                        to = acc[bank][0:TS, j * F:(j + 1) * F]
                        tc_ = slice(t * TS, (t + 1) * TS)
                        if lay == 0:
                            nc.tensor.matmul(to, neT[:, tc_], wnT[:, :], start=True, stop=False)
                            nc.tensor.matmul(to, xT[:, tc_], wsT[:, :], start=False, stop=False)
                            last = nc.tensor.matmul(to, ones[0:2, 0:TS], brow1[:, :], start=False, stop=True)
                        elif lay == 1:
                            for k in range(KH):
                                nc.tensor.matmul(to, h2[:, k, j * TS:(j + 1) * TS], w3s[:, k, :], start=k == 0, stop=False)
                            last = nc.tensor.matmul(to, ones[0:1, 0:TS], brow3[:, :], start=False, stop=True)
                        else:
                            nc.tensor.matmul(to, neT[:, tc_], w4s[:, :], start=True, stop=False)
                            last = nc.tensor.matmul(to, esum[TS:128, tc_], wext[TS:128, :], start=False, stop=True)
                    last.then_inc(blk_ready, 1)

        @block.scalar
        def _(act):
            act.wait_ge(prep_in, 1)
            nc.scalar.copy(w0T[:, :], acc[0][:, 0:F]).then_inc(prep_out, 1)
            act.wait_ge(prep_in, 2)
            nc.scalar.copy(wcat[:, 0:F], w0s[:, :])
            nc.scalar.copy(wcat[:, F:F + 2 * HEADS], acc[1][:, 0:2 * HEADS]).then_inc(prep_out, 1)
            act.wait_ge(prep_in, 4)
            nc.scalar.copy(wnT[:, :], acc[2][:, 0:F]).then_inc(prep_out, 1)
            nc.scalar.copy(wsT[:, :], acc[3][:, 0:F]).then_inc(prep_out, 1)

            def copy_xT(first):
                for q in range(NB):
                    n = min(NPAD - q * BW, BW)
                    act.wait_ge(xT_in, first + q + 1)
                    nc.scalar.copy(xT[:, q * BW:q * BW + n], acc[q % 8][:, 0:n]).then_inc(xT_ready, 1)

            copy_xT(0)
            for t in range(NT):
                if t and t % TT == 0:
                    act.wait_ge(piece_done, 16 * (t // TT))
                act.wait_ge(prep_in, 4 + t + 1)
                ins = nc.scalar.copy(tpiece[:, t % TT, :], acc[t % 4][0:TS, 0:TW])
                if t % TT == TT - 1:
                    ins.then_inc(piece_ready, 1)
                nc.scalar.copy(ssrc[:, t, :], acc[t % 4][0:TS, TW:TW + HEADS]).then_inc(prep_out, 1)

            act.wait_ge(ld_e16, 32)

            def edge_logits(i):
                nc.scalar.copy(ein[:, :], ea16s[:, ds(i * 512, 512)]).then_inc(ein_ready, 1)
                act.wait_ge(eT_in, i + 1)
                nc.scalar.copy(eT[:, :], acc[5][:, 0:4 * EP]).then_inc(eT_out, 1)
                act.wait_ge(el_in, i + 1)
                nc.scalar.copy(rec[:, ds(i * 32, 32), R_EA:R_EA + HEADS],
                               acc[6][0:EP, 0:128].rearrange("p (c h) -> p c h", h=HEADS)).then_inc(el_out, 1)

            with act.Fori(0, EC // 32) as i:
                edge_logits(i)

            def exp_group(i, k):
                act.wait_ge(shifted, i * UN + k + 1)
                nc.scalar.activation(smalls[:, k % 2, 16:32], smalls[:, k % 2, 0:16], ACT.Exp).then_inc(exped, 1)

            def copy_stat(i, k):
                act.wait_ge(turned, i * UN + k + 1)
                s = (k % UN) * GR
                nc.scalar.copy(dT[:, s:s + GR, :], psT[:, :, :]).then_inc(dT_ready, 1)
                if not (isinstance(i, int) and i * UN + k < UN):
                    act.wait_ge(main_done, (i * UN + k) * GR - (UN - 1) * GR)
                nc.scalar.copy(statf[:, s:s + GR, :], stat[:, s:s + GR, 0:TS]).then_inc(statf_ready, 1)

            def check_tile(i, k, chunks):
                for j in chunks:
                    c = (i * UN + k) * GR + j
                    now = act.value_load(tmap[0:1, 0, ds(c, 1)], min_val=0, max_val=NT)
                    then = act.value_load(tmap[0:1, 0, ds(c + 1, 1)], min_val=0, max_val=NT)
                    with act.If(now != then):
                        tile = act.value_load(tmap[0:1, 1, ds(c, 1)], min_val=0, max_val=NT - 1)
                        act.wait_ge(main_done, c + 1)
                        act.wait_ge(stage_free, tile + 1)
                        for b, (at, n) in enumerate(DB):
                            nc.scalar.copy(stage[:, ds((tile % 2) * DW + at, n)], acc[b][0:TS, 0:n])
                        nc.scalar.copy(ys[0:TS, ds(tile, 1), :].rearrange("p t f -> p (t f)"), acc[6][0:TS, HCOL:HCOL + F]).then_inc(act_step, 1)
                        act.wait_ge(act_step, tile + 1)
                        for b in range(7):
                            n = BANK if b < 6 else HCOL + F
                            last = nc.scalar.copy(acc[b][0:TS, 0:n], zerow[0:TS, 0:n])
                        last.then_inc(evac_done, 1)

            def turn(i, last=False):
                for k in range(UN):
                    if not (last and k + 1 >= UN):
                        exp_group(i, k + 1)
                    check_tile(i, k, (0,))
                    if not (last and k + 2 >= UN):
                        copy_stat(i, k + 2)
                    check_tile(i, k, (1, 2, 3))

            act.wait_ge(maps_ready, 1)
            act.sem_inc(evac_done, 1)
            copy_stat(0, 0)
            exp_group(0, 0)
            copy_stat(0, 1)
            turn(0)
            with act.Fori(1, TURNS - 1) as i:
                turn(i)
            turn(TURNS - 1, last=True)
            act.wait_ge(main_done, NC)
            for b, (at, n) in enumerate(DB):
                last = nc.scalar.copy(esum[TS:128, at:at + n], acc[b][TS:128, 0:n])
            last.then_inc(esum_ready, 1)

            act.wait_ge(elu_in, 1)
            nc.scalar.activation(scr, scr, ACT.Exp).then_inc(elu_exp, 1)
            for lay in range(4):
                act.wait_ge(root_in, lay + 1)
                nc.scalar.activation(st[0:TS, 1, :], st[0:TS, 0, :], ACT.Sqrt).then_inc(root_out, 1)
                if lay == 3:
                    break
                act.wait_ge(x_ready, lay + 1)
                nc.scalar.mul(xh, xr, XS).then_inc(xh_ready, 1)
                if lay < 2:
                    copy_xT(NB * (lay + 1))
                if lay != 1:
                    act.wait_ge(tile_used, NT * (lay + 1))
                    for b, (at, n) in enumerate(DB):
                        nc.scalar.mul(neT[:, at:at + n], acc[b][:, 0:n], 1.0 / XS).then_inc(neigh_out, 1)
                else:
                    for q in range(NB):
                        n = min(NPAD - q * BW, BW)
                        at = 9 * q
                        act.wait_ge(mlp_in, at + 1)
                        nc.scalar.activation(h0[:, 0:n], acc[7][:, 0:n], ACT.Relu, bias=bcol[:, 0:1]).then_inc(mlp_out, 1)
                        for m in range(KH):
                            act.wait_ge(mlp_in, at + 2 + m)
                            nc.scalar.activation(h1[:, m, 0:n], acc[m][:, 0:n], ACT.Tanh, bias=bcol[:, 1 + m:2 + m]).then_inc(mlp_out, 1)
                        for m in range(KH):
                            act.wait_ge(mlp_in, at + 6 + m)
                            nc.scalar.activation(h2[:, m, 0:n], acc[4 + m][:, 0:n], ACT.Tanh, bias=bcol[:, 1 + KH + m:2 + KH + m]).then_inc(mlp_out, 1)

        @block.vector
        def _(dve):
            step = Steps(dve, dve_step)
            V = nc.vector
            V.memset(zerow[:, :], 0.0).then_inc(zero_ready, 1)
            step.done(V.memset(esum[:, DW:NPAD], 0.0))
            dve.wait_ge(ld_ends, 64)
            step.done(V.tensor_copy(rec[:, :, R_DST].bitcast(I32), dsti))
            step.done(V.tensor_scalar(rec[:, :, R_DC], dsti, float(-CEN), None, ALU.add))
            step.done(V.tensor_copy(srcf, srci))
            step(V.tensor_scalar(pos.bitcast(I32), srci, 5, None, ALU.logical_shift_right))
            step(V.tensor_scalar(tidf, pos.bitcast(I32), 1.0 / 3, -1.0 / 3, ALU.mult, ALU.add))
            step(V.tensor_scalar(tidf, tidf, RNE, None, ALU.add))
            step(V.tensor_scalar(tidf, tidf, -RNE, None, ALU.add))
            step(V.scalar_tensor_tensor(rec[:, :, R_SL], tidf, float(-TS), srcf, ALU.mult, ALU.add))
            step.done(V.memset(zero, 0.0))
            step(V.memset(pos, 0.0))
            dve.wait_ge(consts, 2)
            for b in range(NT):
                step(V.tensor_scalar(mask, tidf, binid[0:EP, b:b + 1], 0.0, ALU.is_equal, ALU.add, accum_out=bins[0:EP, 0, b:b + 1]))
            V.tensor_copy(bins[0:EP, 1, :], bins[0:EP, 0, :]).then_inc(totals_ready, 1)
            dve.wait_ge(prefix_in, 1)
            step(V.tensor_scalar(bins[:, 2, :], acc[4][:, 64:64 + NT], float(CH - 1), None, ALU.add))
            step(V.tensor_copy(binsi[:, :], bins[:, 2, :]))
            step(V.tensor_scalar(binsi[:, :], binsi[:, :], 7, None, ALU.logical_shift_right))
            step(V.tensor_copy(bins[:, 3, :], binsi[:, :]))
            step(V.tensor_scalar(bins[:, 3, :], bins[:, 3, :], 1.0, None, ALU.max))
            step(V.memset(bins[:, 5, :], 0.0))
            step(V.tensor_tensor_scan(bins[:, 4, :], bins[:, 3, :], bins[:, 5, :], 0.0, ALU.add, ALU.add))
            step(V.tensor_tensor(bins[:, 6, :], bins[:, 4, :], bins[:, 3, :], ALU.subtract))
            step(V.tensor_scalar(bins[:, 6, :], bins[:, 6, :], float(CH), -1.0, ALU.mult, ALU.add))
            V.tensor_tensor(bins[0:EP, 7, :], bins[0:EP, 6, :], acc[4][0:EP, 0:NT], ALU.add).then_inc(offs_read, 1)
            dve.wait_ge(offs_read, 1)
            for b in range(NT):
                step(V.tensor_scalar(mask, tidf, binid[0:EP, b:b + 1], None, ALU.is_equal))
                step(V.tensor_tensor_scan(cum, mask, zero, bins[0:EP, 7, b:b + 1], ALU.add, ALU.add))
                step(V.tensor_tensor(cum, cum, mask, ALU.mult))
                step(V.tensor_tensor(pos, pos, cum, ALU.add))
            step(V.tensor_copy(posi, pos))
            step.done(V.tensor_scalar(parti, posi, CH - 1, None, ALU.bitwise_and))
            step(V.tensor_scalar(mask.bitcast(I32), posi, 7, None, ALU.logical_shift_right))
            step(V.tensor_copy(srcf, mask.bitcast(I32)))
            step(V.tensor_copy(tidf, parti))
            step(V.scalar_tensor_tensor(pos, tidf, float(NC), srcf, ALU.mult, ALU.add))
            V.tensor_copy(posi, pos).then_inc(rank_done, 1)
            dve.wait_ge(prep_out, 4 + NT)
            for part in range(3):
                step(V.tensor_copy(s3[:, :, :, part], ssrc[:, :, :]))
                if part < 2:
                    step(V.tensor_tensor(ssrc[:, :, :], ssrc[:, :, :], s3[:, :, :, part], ALU.subtract))
            step(V.memset(mf[:, 0, :], 0.0))
            dve.wait_ge(chunk_ids, 1)
            for b in range(NT):
                step(V.scalar_tensor_tensor(mf[:, 0, :], mf[:, 1, :], bins[0:1, 4, b:b + 1], mf[:, 0, :], ALU.is_ge, ALU.add))
            step.done(V.tensor_copy(tmap[:, 0, :], mf[:, 0, :]))
            step(V.tensor_scalar(tmap[:, 1, :], mf[:, 0, :], float(NT - 1), None, ALU.min))
            step(V.memset(stat[:, :, :], 0.0))
            V.memset(stat[:, :, OCOL:OCOL + 2], 1.0).then_inc(maps_ready, 1)
            dve.wait_ge(maps_ready, 1)
            dve.wait_ge(consts, 3)
            dve.wait_ge(recs_in, 16)

            def stat_group(i, k):
                s = (k % UN) * GR
                if not (isinstance(i, int) and i * UN + k < UN):
                    dve.wait_ge(main_done, (i * UN + k) * GR - (UN - 1) * GR)
                for j in range(GR):
                    c = (i * UN + k) * GR + j
                    V.tensor_scalar(stat[:, s + j, 0:TS], iotas[:, :], recs[:, ds(c, 1), R_SL:R_SL + 1].rearrange("p c w -> p (c w)"),
                                    None, ALU.is_equal)
                V.tensor_copy(stat[:, s:s + GR, TS:OCOL],
                              recsb[:, ds((i * UN + k) * GR, GR), 2 * R_E6:2 * R_E6 + E6C]).then_inc(stat_ready, 1)

            def logits(i, k):
                z = smalls[:, k % 2, 0:16]
                z3 = z.rearrange("p (j h) -> p j h", h=HEADS)
                dve.wait_ge(src_logits, i * UN + k + 1)
                V.tensor_reduce(z, psS[:, :].rearrange("p (a b) -> p a b", b=3), AX, ALU.add).then_inc(looked, 1)
                dve.wait_ge(looked, i * UN + k + 1)
                step(V.tensor_tensor(z3, z3, recs[:, ds((i * UN + k) * GR, GR), R_EA:R_EA + HEADS], ALU.add))
                s = (k % UN) * GR
                for j in range(GR):
                    dve.wait_ge(gathered[s + j], (i + k // UN) * 16 + 16)
                step(V.tensor_tensor(z3, z3, gt[:, s:s + GR, F:TW], ALU.add))
                step(V.scalar_tensor_tensor(z, z, ALPHA, z, ALU.mult, ALU.max))
                m = smalls[:, k % 2, 32:36]
                step(V.tensor_reduce(m, z3, AX, ALU.max))
                V.tensor_tensor(z3, z3, m.rearrange("p (j a) -> p j a", a=1).to_broadcast([128, GR, HEADS]), ALU.subtract).then_inc(shifted, 1)

            def messages(i, k):
                e = smalls[:, k % 2, 16:32]
                e3 = e.rearrange("p (j h) -> p j h", h=HEADS)
                m = smalls[:, k % 2, 36:40]
                s = (k % UN) * GR
                dve.wait_ge(exped, i * UN + k + 1)
                step(V.tensor_reduce(m, e3, AX, ALU.add))
                step(V.reciprocal(m, m))
                step(V.tensor_tensor(e3, e3, m.rearrange("p (j a) -> p j a", a=1).to_broadcast([128, GR, HEADS]), ALU.mult))
                if not (isinstance(i, int) and i * UN + k < 2):
                    dve.wait_ge(main_done, (i * UN + k) * GR - GR)
                to = msg[:, (k % 2) * GR:(k % 2) * GR + GR, :].rearrange("p j (h d) -> p j h d", h=HEADS)
                frm = gt[:, s:s + GR, 0:F].rearrange("p j (h d) -> p j h d", h=HEADS)
                at4 = e3.rearrange("p j (h a) -> p j h a", a=1).to_broadcast([128, GR, HEADS, HF])
                V.tensor_tensor(to, frm, at4, ALU.mult).then_inc(msg_ready, 1)

            def one_hot(i, k, j):
                c = (i * UN + k) * GR + j
                if not (isinstance(i, int) and c < GR):
                    dve.wait_ge(main_done, c - (GR - 1))
                V.tensor_scalar(hot[j], iotad[:, :], recs[:, ds(c, 1), R_DC:R_DC + 1].rearrange("p c w -> p (c w)"),
                                None, ALU.is_equal).then_inc(hot_ready, 1)

            PER_TURN = 7 * UN

            def turn(i, last=False):
                for k in range(UN):
                    if not (last and k + 1 >= UN):
                        logits(i, k + 1)
                    one_hot(i, k, 0)
                    one_hot(i, k, 1)
                    if not (last and k + 1 >= UN):
                        messages(i, k + 1)
                    one_hot(i, k, 2)
                    if not (last and k + 3 >= UN):
                        stat_group(i, k + 3)
                    one_hot(i, k, 3)

            for k in range(3):
                stat_group(0, k)
            logits(0, 0)
            messages(0, 0)
            turn(0)
            before = step.n
            with dve.Fori(1, TURNS - 1) as i:
                step.at = i * PER_TURN - PER_TURN
                turn(i)
                assert step.n == before + PER_TURN
            step.at = 0
            step.n = before + PER_TURN * (TURNS - 2)
            turn(TURNS - 1, last=True)

            dve.wait_ge(evac_done, NT + 1)
            dve.wait_ge(esum_ready, 1)
            step.done(V.memset(neT[:, DW:NPAD], 0.0))
            V.tensor_scalar(scr, yr, 0.0, None, ALU.min).then_inc(elu_in, 1)
            dve.wait_ge(elu_in, 1)
            step(V.scalar_tensor_tensor(yr, yr, 0.0, xr, ALU.max, ALU.add))
            dve.wait_ge(elu_exp, 1)
            step(V.scalar_tensor_tensor(yr, scr, -1.0, yr, ALU.add, ALU.add))

            def wide(v):
                return v.rearrange("p (t a) -> p t a", a=1).to_broadcast([TS, NT, F])

            def norm():
                step(V.tensor_reduce(st[0:TS, 0, :], yr, AX, ALU.add))
                step(V.tensor_scalar(st[0:TS, 0, :], st[0:TS, 0, :], -1.0 / F, None, ALU.mult))
                step(V.tensor_tensor(xr, yr, wide(st[0:TS, 0, :]), ALU.add))
                step(V.tensor_tensor(yr, xr, xr, ALU.mult))
                step(V.tensor_reduce(st[0:TS, 0, :], yr, AX, ALU.add))
                V.tensor_scalar(st[0:TS, 0, :], st[0:TS, 0, :], 1.0 / F, EPS, ALU.mult, ALU.add).then_inc(root_in, 1)

            for lay in range(4):
                norm()
                dve.wait_ge(root_out, lay + 1)
                step(V.reciprocal(st[0:TS, 2, :], st[0:TS, 1, :]))
                V.tensor_tensor(xr, xr, wide(st[0:TS, 2, :]), ALU.mult).then_inc(x_ready, 1)
                if lay == 3:
                    break
                dve.wait_ge(x_ready, lay + 1)
                dve.wait_ge(xh_ready, lay + 1)
                V.scalar_tensor_tensor(xl, xr, XS, xh, ALU.mult, ALU.subtract).then_inc(halves_ready, 1)
                if lay == 0:
                    dve.wait_ge(deg_in, 1)
                    for b, (at, n) in enumerate(DB):
                        last = V.tensor_scalar(rdeg[:, at:at + n], acc[b][:, 0:n], 1.0, None, ALU.max)
                    last.then_inc(deg_out, 1)
                    dve.wait_ge(deg_out, 1)
                    step(V.reciprocal(rdeg[:, 0:DW], rdeg[:, 0:DW]))
                if lay == 1:
                    dve.wait_ge(tile_used, NT * 2)
                    for b, (at, n) in enumerate(DB):
                        V.scalar_tensor_tensor(neT[:, at:at + n], acc[b][:, 0:n], 1.0 / XS, rdeg[:, at:at + n],
                                               ALU.mult, ALU.mult).then_inc(neigh_out, 1)
                for q in range(NB):
                    n = min(NT - q * BT, BT)
                    dve.wait_ge(blk_ready, NB * lay + q + 1)
                    ps = acc[0 if lay == 1 else q % 8][0:TS, 0:n * F]
                    yb, xb = (v[0:TS, q * BT:q * BT + n, :].rearrange("p t f -> p (t f)") for v in (ys, xs))
                    if lay < 2:
                        V.tensor_tensor(yb, ps, xb, ALU.add).then_inc(blk_used, 1)
                    else:
                        V.scalar_tensor_tensor(yb, ps, 0.0, xb, ALU.max, ALU.add).then_inc(blk_used, 1)
                dve.wait_ge(blk_used, NB * (lay + 1))
    return nc


_INS = ['x', 'src', 'dst', 'edge_attr_16', 'edge_attr_6', 'L0_gnn_W', 'L0_gnn_a', 'L1_gnn_W_neigh', 'L1_gnn_b_neigh',
        'L1_gnn_W_self', 'L1_gnn_b_self', 'L2_gnn_Wg', 'L2_gnn_Ws', 'L2_gnn_bg', 'L2_gnn_W1', 'L2_gnn_b1', 'L2_gnn_W2',
        'L2_gnn_b2', 'L2_gnn_W3', 'L2_gnn_b3', 'L3_gnn_W', 'L3_gnn_b', 'L3_gnn_We', 'L3_gnn_be']


def kernel(**inputs):
    import numpy as _np
    import concourse.bacc as _bacc
    from concourse import mybir as _mybir
    from concourse.bass_utils import run_bass_kernel_spmd as _run

    nc = _bacc.Bacc("TRN2", target_bir_lowering=False, num_devices=1)
    arrays, args = {}, []
    for name in _INS:
        a = _np.ascontiguousarray(inputs[name])
        arrays[f"in_{name}"] = a
        args.append(nc.dram_tensor(f"in_{name}", a.shape, _mybir.dt.from_np(a.dtype), kind="ExternalInput").ap())
    args.append(nc.dram_tensor("out", (N, F), FP32, kind="ExternalOutput").ap())
    gnn_stack(nc, *args)
    r = _run(nc, [arrays], core_ids=[0])
    return r.results[0]["out"]
```

```python
import concourse.bass as bass
from concourse import mybir
from contextlib import ExitStack

FP32 = mybir.dt.float32
BF16 = mybir.dt.bfloat16
FP16 = mybir.dt.float16
I32 = mybir.dt.int32
ALU = mybir.AluOpType
ACT = mybir.ActivationFunctionType
AX = mybir.AxisListType.X
ds = bass.ds

N = 3125
E = 100000
F = 128
HEADS, HF = 4, 32
EF0, EF3 = 16, 6
HID = 512
KH = HID // F

TS = 96
NT = -(-N // TS)
LAST = N - TS * (NT - 1)
NPAD = NT * TS
EP, EC = 125, 800
CH = 128
GR = 4
UN = 4
NBIN = 2 * NT
NC = -(-(E // CH + NBIN) // (GR * UN)) * GR * UN
NG = NC // GR
SLOTS = GR * UN
BANK = 512
DW = 3136
DB = [(b * BANK, min(BANK, DW - b * BANK)) for b in range(-(-DW // BANK))]
HB = 3
LOW = HB * BANK
HW_ = DW - LOW
BLOCKS = [64, 96, 160, 240, 240]
W = 16
R_DST, R_DC, R_SL, R_EA, R_E6 = 0, 1, 2, 3, 7
TW = F + HEADS
E6C = 3 * EF3
OCOL = TS + E6C
HCOL = 64
FAR = 20000.0
XS = 4096.0
ALPHA = 0.2
EPS = 1e-5
RNE = 12582912.0
AR = 4
BT = 4
NB = -(-NT // BT)


class Steps:

    def __init__(self, eng, sem):
        self.eng, self.sem, self.n, self.at = eng, sem, 0, 0

    def done(self, ins):
        ins.then_inc(self.sem, 1)
        self.n += 1

    def wait(self):
        self.eng.wait_ge(self.sem, self.at + self.n)

    def __call__(self, ins):
        self.done(ins)
        self.wait()


def gnn_stack(nc, x, src, dst, ea16, ea6, W0, a0, Wn, bn, Wsf, bs, Wg, Ws, bg, W1, b1, W2, b2, W3, b3, W4, b4, We, be, out):
    ctx = ExitStack()
    with ctx:
        def sb(name, shape, dt=FP32):
            return ctx.enter_context(nc.sbuf_tensor(name, shape, dt))

        def sem(name):
            return ctx.enter_context(nc.semaphore(name))

        def dram(name, shape, dt=FP32):
            return nc.dram_tensor(name, shape, dt, kind="Internal").ap()

        table = dram("table", [NPAD, TW])
        records = dram("records", [CH * NC, W])
        counts = dram("counts", [NT, TS, DW], FP16)

        arenaA = sb("arenaA", [128, NC * W])
        arenaB = sb("arenaB", [128, EC * W])
        arenaC = sb("arenaC", [128, 6 * EC + 500])
        ident = sb("ident", [128, 128])
        identb = sb("identb", [128, 128], BF16)
        ones = sb("ones", [128, 128])
        zerob = sb("zerob", [128, 128], BF16)
        tril = sb("tril", [128, 128])
        degsel = sb("degsel", [128, F])
        iotad = sb("iotad", [128, HW_], FP16)
        iotas = sb("iotas", [128, TS], BF16)
        binid = sb("binid", [128, NBIN])
        xs = sb("xs", [128, NT, F])
        ys = sb("ys", [128, NT, F])
        arenaD = sb("arenaD", [128, 2 * NPAD])
        xT, esum = arenaD[:, 0:NPAD], arenaD[:, NPAD:2 * NPAD]
        w0s = sb("w0s", [F, F])
        w0T = sb("w0T", [F, F])
        ablk = sb("ablk", [F, 2 * HEADS])
        edgeblk = sb("edgeblk", [128, 8 * HEADS])
        wcat = sb("wcat", [F, F + 2 * HEADS])
        wnT = sb("wnT", [F, F])
        wsT = sb("wsT", [F, F])
        wgs = sb("wgs", [F, 2, F])
        w4s = sb("w4s", [F, F])
        wext = sb("wext", [128, F])
        brow1 = sb("brow1", [2, F])
        brow3 = sb("brow3", [1, F])
        bcol = sb("bcol", [F, 1 + 2 * KH])
        ssrc = sb("ssrc", [TS, NT, HEADS])
        s3 = sb("s3", [TS, NT, HEADS, 3], BF16)
        bins = sb("bins", [128, 6, NBIN])
        carry = sb("carry", [EP, NBIN])
        binsi = sb("binsi", [128, NBIN], I32)
        tmap = sb("tmap", [1, NG], I32)
        st = sb("st", [128, 3, NT])
        places = sb("places", [EP, 2, SLOTS], I32)
        rowid = sb("rowid", [128, 2, SLOTS], I32)
        smalls = sb("smalls", [128, 2, 48])

        ea16s = arenaA[0:EP, 0:EC * EF0]
        rec = arenaB[0:EP, :].rearrange("p (c w) -> p c w", w=W)
        recb = arenaB[0:EP, :].bitcast(BF16).rearrange("p (c w) -> p c w", w=2 * W)
        parts = [arenaC[0:EP, k * EC:(k + 1) * EC] for k in range(6)]
        srci, dsti = parts[0].bitcast(I32), parts[1].bitcast(I32)
        srcf, half, tidf, work, pos = parts[0], parts[1], parts[2], parts[3], parts[4]
        posi = parts[5].bitcast(I32)
        MB = max(BLOCKS)
        binb = parts[0][:, 0:EC // 2].bitcast(BF16)
        masks = [parts[0][:, EC // 2 + k * MB // 2:EC // 2 + (k + 1) * MB // 2] for k in range(2)]
        cums = [parts[1][:, k * MB:(k + 1) * MB] for k in range(2)]
        zero = parts[2][:, 0:MB]
        whole = [parts[2][:, (k + 1) * MB:(k + 2) * MB].bitcast(I32) for k in range(2)]
        eT = arenaC[:, 6 * EC:6 * EC + 4 * EP]
        ein = xT[0:EP, 0:512]
        batch = xT[0:EP, 512:512 + 2 * SLOTS * W].rearrange("p (h s w) -> p h s w", h=2, s=SLOTS)
        HE = EC // 2 * EF3
        ysflat = ys[:, :, :].rearrange("p t f -> p (t f)")
        e6h = [ysflat[0:EP, 0:HE], esum[0:EP, 0:HE]]
        TP = 3
        TT = NT // TP
        tpiece = ysflat[0:TS, HE:HE + TT * TW].rearrange("p (t w) -> p t w", w=TW)
        SC = (NPAD - HE) // W
        PADS = -(-NC // SC)
        sent = esum[:, HE:HE + SC * W].rearrange("p (c w) -> p c w", w=W)
        mf = arenaC[0:NT, 0:3 * (NC + 1)].rearrange("p (k c) -> p k c", k=3)
        s3T = arenaC[0:NT, 3 * (NC + 1):3 * (NC + 1) + 6 * TS].bitcast(BF16).rearrange("p (k s) -> p k s", k=12)
        assert 3 * (NC + 1) + 6 * TS <= 5 * EC
        inTile = arenaC[0:NT, 6 * EC:6 * EC + NC // 2].bitcast(BF16)
        endc = bins[0:NT, 0, 0:2]
        beside = bins[0:NT, 1, 0:NT]
        recs = arenaA[:, :].rearrange("p (c w) -> p c w", w=W)
        recsb = arenaA[:, :].bitcast(BF16).rearrange("p (c w) -> p c w", w=2 * W)
        hot = [arenaB[:, s * HW_ // 2:(s + 1) * HW_ // 2].bitcast(FP16) for s in range(2 * GR)]
        o = 2 * GR * HW_ // 2
        stage = arenaB[0:TS, o:o + DW // 2].bitcast(FP16); o += DW // 2
        msg = arenaB[:, o:o + SLOTS * F].rearrange("p (s f) -> p s f", f=F); o += SLOTS * F
        gt = arenaB[:, o:o + SLOTS * TW].rearrange("p (s w) -> p s w", w=TW); o += SLOTS * TW
        assert o <= EC * W
        zerow = arenaC[:, 6 * EC - BANK:6 * EC]
        lut = arenaD[0:TS, 2 * NPAD - NC * 6:2 * NPAD].bitcast(BF16).rearrange("p (c h) -> p c h", h=12)
        o = 0
        stat = arenaC[:, o:o + UN * GR * 64].bitcast(BF16).rearrange("p (s f) -> p s f", f=128); o += UN * GR * 64
        statf = arenaC[:, o:o + UN * GR * TS].rearrange("p (s f) -> p s f", f=TS); o += UN * GR * TS
        dT = arenaC[0:TS, o:o + UN * GR * 64].bitcast(BF16).rearrange("p (s f) -> p s f", f=128); o += UN * GR * 64
        assert o <= 6 * EC
        ring = arenaB[0:TS, 0:AR * DW // 2].bitcast(FP16).rearrange("p (s d) -> p s d", s=AR)
        o = (AR + 1) * DW // 2
        ring0 = arenaB[0:TS, AR * DW // 2:o].bitcast(FP16)
        w1s = arenaB[:, o:o + HID]; o += HID
        w2s = arenaB[:, o:o + KH * HID].rearrange("p (k n) -> p k n", k=KH); o += KH * HID
        w3s = arenaB[:, o:o + KH * F].rearrange("p (k n) -> p k n", k=KH); o += KH * F
        assert o <= EC * W
        scr = arenaA[0:TS, 0:NT * F].rearrange("p (t f) -> p t f", f=F)
        xh = arenaA[0:TS, 0:NT * F // 2].bitcast(FP16).rearrange("p (t f) -> p t f", f=F)
        xl = arenaA[0:TS, NT * F // 2:NT * F].bitcast(FP16).rearrange("p (t f) -> p t f", f=F)
        neT = arenaA[:, NT * F:NT * F + NPAD]
        rdeg = arenaA[:, NT * F + NPAD:NT * F + 2 * NPAD]
        assert NT * F + 2 * NPAD <= NC * W
        BW = BT * TS
        h0 = arenaC[:, 0:BW]
        h1 = arenaC[:, BW:BW * (1 + KH)].rearrange("p (k n) -> p k n", k=KH)
        h2 = arenaC[:, BW * (1 + KH):BW * (1 + 2 * KH)].rearrange("p (k n) -> p k n", k=KH)
        xr, yr = xs[0:TS, :, :], ys[0:TS, :, :]

        acc = [ctx.enter_context(nc.psum_tensor(f"acc{b}", [128, BANK], FP32)) for b in range(8)]
        psT = acc[7][0:TS, 0:256].bitcast(BF16).rearrange("p (j e) -> p j e", j=GR)
        psS = acc[7][:, 256:256 + GR * HEADS * 3]

        ld_ends, ld_x, ld_e16, ld_e6, ld_w, ld_w2, ld_w3 = (
            sem(n) for n in ("ld_ends", "ld_x", "ld_e16", "ld_e6", "ld_w", "ld_w2", "ld_w3"))
        pool_step, pool_passed, consts, sent_done, e6_split = (sem(n) for n in ("pool_step", "pool_passed", "consts", "sent_done", "e6_split"))
        prep_in, prep_out = sem("prep_in"), sem("prep_out")
        piece_ready, piece_done = sem("piece_ready"), sem("piece_done")
        ein_ready, eT_in, eT_out, el_in, el_out = (sem(n) for n in ("ein_ready", "eT_in", "eT_out", "el_in", "el_out"))
        dve_step, act_step, act_passed = sem("dve_step"), sem("act_step"), sem("act_passed")
        totals_ready, prefix_in = (sem(n) for n in ("totals_ready", "prefix_in"))
        maps_ready, recs_in = sem("maps_ready"), sem("recs_in")
        scattered = [sem(f"scattered{h}") for h in range(2)]
        gathered = [sem(f"gathered{s}") for s in range(SLOTS)]
        stat_ready, statf_ready, turned, dT_ready = (sem(n) for n in ("stat_ready", "statf_ready", "turned", "dT_ready"))
        src_logits, looked, shifted, exped, msg_ready = (sem(n) for n in ("src_logits", "looked", "shifted", "exped", "msg_ready"))
        hot_ready, main_done, copied, six_out, six_zero, released = (
            sem(n) for n in ("hot_ready", "main_done", "copied", "six_out", "six_zero", "released"))
        half_out, half_stored, half_free = ([sem(f"{n}{h}") for h in ("low", "high")] for n in ("out_", "stored_", "free_"))
        ranked = sem("ranked")
        lut_in, lut_pe, lut_act = (sem(n) for n in ("lut_in", "lut_pe", "lut_act"))
        offs_read, zero_ready, chunk_ids, esum_ready = (sem(n) for n in ("offs_read", "zero_ready", "chunk_ids", "esum_ready"))
        count_in = [sem(f"count_in{s}") for s in range(AR + 1)]
        elu_in, elu_exp, root_in, root_out, x_ready = (sem(n) for n in ("elu_in", "elu_exp", "root_in", "root_out", "x_ready"))
        xh_ready, halves_ready, xT_in, xT_ready = (sem(n) for n in ("xh_ready", "halves_ready", "xT_in", "xT_ready"))
        tile_used, neigh_out, deg_in, deg_out = (sem(n) for n in ("tile_used", "neigh_out", "deg_in", "deg_out"))
        blk_ready, blk_used, out_done = sem("blk_ready"), sem("blk_used"), sem("out_done")
        mlp_in, mlp_out = sem("mlp_in"), sem("mlp_out")

        TURNS = NG // UN

        def load_codes(eng, i, k):
            word = eng.value_load(tmap[0:1, ds(i * UN + k, 1)], min_val=1 << GR, max_val=((NBIN + 2) << GR) - 1)
            return word // (1 << GR), word % (1 << GR)

        def bit(ends, j):
            return ends // (1 << j) % 2

        def code_of(code, ends, j):
            for before in range(j):
                code = code + bit(ends, before)
            return code
        block = ctx.enter_context(nc.Block())

        @block.sync
        def _(sp):
            for lo, hi in ((0, 112), (112, EP)):
                sp.dma_start(srci[lo:hi, :], src.rearrange("(p c) -> p c", p=EP)[lo:hi, :]).then_inc(ld_ends, 16)
                sp.dma_start(dsti[lo:hi, :], dst.rearrange("(p c) -> p c", p=EP)[lo:hi, :]).then_inc(ld_ends, 16)
            sp.wait_ge(consts, 1)
            sp.dma_start(xs[0:TS, 0:NT - 1, :], x[0:TS * (NT - 1), :].rearrange("(t p) f -> p t f", p=TS)).then_inc(ld_x, 16)
            sp.dma_start(xs[0:LAST, NT - 1, :], x[TS * (NT - 1):N, :]).then_inc(ld_x, 16)
            sp.dma_start(w0s[:, :], W0).then_inc(ld_w, 16)
            for h in range(HEADS):
                for k in range(2):
                    sp.dma_start(ablk[HF * h:HF * h + HF, HEADS * (1 - k) + h:HEADS * (1 - k) + h + 1],
                                 a0[h:h + 1, HF * k:HF * k + HF].rearrange("a d -> d a"), allow_slow_non_contiguous=True).then_inc(ld_w, 16)
            for j in range(8):
                sp.dma_start(edgeblk[EF0 * j:EF0 * j + EF0, HEADS * j:HEADS * j + HEADS],
                             a0[:, 2 * HF:2 * HF + EF0].rearrange("h d -> d h"), allow_slow_non_contiguous=True).then_inc(ld_w, 16)
            for lo, hi in ((0, 112), (112, EP)):
                sp.dma_start(ea16s[lo:hi, :], ea16.rearrange("(p c) d -> p (c d)", p=EP)[lo:hi, :]).then_inc(ld_e16, 16)
                for k in range(2):
                    sp.dma_start(e6h[k][lo:hi, :],
                                 ea6.rearrange("(p c) d -> p (c d)", p=EP)[lo:hi, k * HE:(k + 1) * HE]).then_inc(ld_e6, 16)
            for k in range(PADS):
                n = min(SC, NC - k * SC)
                sp.dma_start(records.rearrange("(p c) w -> p c w", c=NC)[:, k * SC:k * SC + n, :],
                             sent[:, 0:n, :]).then_inc(sent_done, 16)
            for to, frm in ((wnT[:, :], Wn), (wsT[:, :], Wsf),
                            (wgs[:, 0, :], Wg), (wgs[:, 1, :], Ws), (w4s[:, :], W4),
                            (brow1[0:1, :], bn.rearrange("(a f) -> a f", a=1)),
                            (brow1[1:2, :], bs.rearrange("(a f) -> a f", a=1)),
                            (brow3[0:1, :], b3.rearrange("(a f) -> a f", a=1)),
                            (bcol[:, 0:1], bg.rearrange("(p a) -> p a", a=1)),
                            (bcol[:, 1:1 + KH], b1.rearrange("(k p) -> p k", p=F)),
                            (bcol[:, 1 + KH:1 + 2 * KH], b2.rearrange("(k p) -> p k", p=F)),
                            (wext[TS:TS + EF3, :], We), (wext[TS + EF3:TS + 2 * EF3, :], We),
                            (wext[TS + 2 * EF3:OCOL, :], We),
                            (wext[OCOL:OCOL + 1, :], b4.rearrange("(a f) -> a f", a=1)),
                            (wext[OCOL + 1:OCOL + 2, :], be.rearrange("(a f) -> a f", a=1))):
                sp.dma_start(to, frm, allow_slow_non_contiguous=True).then_inc(ld_w2, 16)
            for k in range(TP):
                sp.wait_ge(piece_ready, k + 1)
                sp.dma_start(table[k * TT * TS:(k + 1) * TT * TS, :].rearrange("(t p) f -> p t f", p=TS),
                             tpiece).then_inc(piece_done, 16)
            for h in range(2):
                sp.wait_ge(scattered[h], 8 * EC)
            sp.dma_start(arenaA[:, :], records.rearrange("(p c) w -> p (c w)", c=NC)).then_inc(recs_in, 16)
            for h in range(2):
                sp.sem_inc(half_free[h], 1)
            with sp.Fori(0, NT) as t:
                for h, (lo, hi) in enumerate(((0, LOW), (LOW, DW))):
                    sp.wait_ge(half_out[h], t + 1)
                    sp.dma_start(counts[ds(t, 1), :, lo:hi].rearrange("t p d -> p (t d)"), stage[:, lo:hi]).then_inc(half_stored[h], 16)
                    sp.wait_ge(half_stored[h], t * 16 + 16)
                    sp.sem_inc(half_free[h], 1)
            sp.wait_ge(main_done, NC)
            sp.wait_ge(msg_ready, NG)
            for to, frm in ((w1s, W1), (w2s, W2.rearrange("(k p) n -> p k n", p=F)), (w3s, W3.rearrange("(k p) n -> p k n", p=F))):
                sp.dma_start(to, frm).then_inc(ld_w3, 16)
            for lay in range(3):
                if lay:
                    sp.wait_ge(tile_used, NT * lay)
                sp.dma_start(ring0, counts[0, :, :]).then_inc(count_in[AR], 16)
                for s in range(AR):
                    sp.dma_start(ring[:, s, :], counts[1 + s, :, :]).then_inc(count_in[s], 16)
                with sp.Fori(1, (NT - 1) // AR) as i:
                    for s in range(AR):
                        sp.wait_ge(tile_used, i * AR + (NT * lay + 2 + s - AR))
                        sp.dma_start(ring[:, s, :],
                                     counts[ds(i * AR + (1 + s), 1), :, :].rearrange("t p d -> p (t d)")).then_inc(count_in[s], 16)
            sp.wait_ge(x_ready, 4)
            sp.dma_start(out[0:TS * (NT - 1), :].rearrange("(t p) f -> p t f", p=TS), xs[0:TS, 0:NT - 1, :]).then_inc(out_done, 16)
            sp.dma_start(out[TS * (NT - 1):N, :], xs[0:LAST, NT - 1, :]).then_inc(out_done, 16)
            sp.wait_ge(out_done, 32)

        @block.gpsimd
        def _(pool):
            step = Steps(pool, pool_step)
            step.done(nc.gpsimd.memset(xs[:, NT - 1, :], 0.0))
            step.done(nc.gpsimd.memset(ablk[:, :], 0.0))
            step.done(nc.gpsimd.memset(wext[:, :], 0.0))
            step.done(nc.gpsimd.memset(sent[:, :, :], 0.0))
            step(nc.gpsimd.memset(edgeblk[:, :], 0.0))
            step(nc.gpsimd.memset(sent[:, :, R_DC:R_SL + 1], FAR))
            nc.gpsimd.memset(zerob[:, :], 0.0).then_inc(consts, 1)
            step.done(nc.gpsimd.memset(ones[:, :], 1.0))
            step.done(nc.gpsimd.memset(ident[:, :], 0.0))
            step.done(nc.gpsimd.memset(degsel[:, :], 0.0))
            step(nc.gpsimd.memset(tril[:, :], 1.0))
            step.done(nc.gpsimd.affine_select(out=tril[:, :], in_=tril[:, :], compare_op=ALU.is_gt, fill=0.0,
                                              base=0, pattern=[[1, 128]], channel_multiplier=-1))
            step.done(nc.gpsimd.affine_select(out=degsel[:, :], in_=degsel[:, :], compare_op=ALU.not_equal, fill=1.0,
                                              base=-OCOL, pattern=[[0, F]], channel_multiplier=1))
            step.done(nc.gpsimd.iota(binid[:, :], pattern=[[1, NBIN]], base=0, channel_multiplier=0,
                                     allow_small_or_imprecise_dtypes=True))
            step(nc.gpsimd.affine_select(out=ident[:, :], in_=ident[:, :], compare_op=ALU.not_equal, fill=1.0,
                                         base=0, pattern=[[-1, 128]], channel_multiplier=1))
            nc.gpsimd.tensor_copy(identb[:, :], ident[:, :]).then_inc(consts, 1)
            step.done(nc.gpsimd.iota(iotad[:, :], pattern=[[1, HW_]], base=0, channel_multiplier=0,
                                     allow_small_or_imprecise_dtypes=True))
            step(nc.gpsimd.iota(iotas[:, :], pattern=[[1, TS]], base=0, channel_multiplier=0,
                                     allow_small_or_imprecise_dtypes=True))
            pool.sem_inc(consts, 1)
            pool.wait_ge(ld_e6, 64)
            for k in range(2):
                e = e6h[k].rearrange("p (c d) -> p c d", d=EF3)
                to = recb[:, k * (EC // 2):(k + 1) * (EC // 2), :]
                for part in range(3):
                    at = 2 * R_E6 + EF3 * part
                    step(nc.gpsimd.tensor_copy(to[:, :, at:at + EF3], e))
                    if part < 2:
                        step(nc.gpsimd.tensor_tensor(e, e, to[:, :, at:at + EF3], ALU.subtract))
            pool.wait_ge(sent_done, 16 * PADS)
            HALF = SLOTS

            def scatter(i):
                for h in range(2):
                    c0 = i * (2 * HALF) + h * HALF
                    if not (isinstance(i, int) and i == 0):
                        pool.wait_ge(scattered[h], i * (16 * HALF))
                    step.done(nc.gpsimd.tensor_copy(places[:, h, :], posi[:, ds(c0, HALF)]))
                    step(nc.gpsimd.tensor_copy(batch[:, h, :, :], rec[:, ds(c0, HALF), :]))
                    pool.sem_inc(pool_passed, 1)
                    for s in range(HALF):
                        nc.gpsimd.indirect_dma_start(
                            out=records, out_offset=bass.IndirectOffsetOnAxis(ap=places[:, h, s:s + 1], axis=0),
                            in_=batch[:, h, s, :], in_offset=None).then_inc(scattered[h], 16)
            start = 0
            before = step.n
            for blk, cols in enumerate(BLOCKS):
                pool.wait_ge(ranked, blk + 1)
                pool.wait_ge(el_out, (start + cols) // 32)
                if start + cols == EC:
                    nc.gpsimd.iota(mf[:, 1, :], pattern=[[1, NC + 1]], base=0, channel_multiplier=0,
                                   allow_small_or_imprecise_dtypes=True).then_inc(chunk_ids, 1)
                first, end = start // (2 * HALF), (start + cols) // (2 * HALF)
                if blk == 0:
                    scatter(0)
                    first = 1
                step.n = before + 4
                with pool.Fori(first, end) as i:
                    step.at = i * 4 - 4
                    scatter(i)
                start += cols
            step.at = 0
            step.n = before + 2 * (EC // HALF)
            pool.wait_ge(recs_in, 16)
            pool.wait_ge(piece_done, 16 * TP)

            def row_ids(i, half):
                step(nc.gpsimd.tensor_copy(
                    rowid[:, half, :],
                    recs[:, ds(i * SLOTS, SLOTS), R_DST:R_DST + 1].rearrange("p c w -> p (c w)").bitcast(I32)))
                pool.sem_inc(pool_passed, 1)

            def gather(k, half):
                for s in range(k * GR, (k + 1) * GR):
                    nc.gpsimd.indirect_dma_start(
                        out=gt[:, s, :], out_offset=None, in_=table,
                        in_offset=bass.IndirectOffsetOnAxis(ap=rowid[:, half, s:s + 1], axis=0)).then_inc(gathered[s], 16)

            def gathers(i, half):
                row_ids(i, half)
                for k in range(UN):
                    pool.wait_ge(msg_ready, i * UN + (k + 1 - UN))
                    pool.sem_inc(pool_passed, 1)
                    gather(k, half)

            row_ids(0, 0)
            for k in range(UN):
                gather(k, 0)
            with pool.Fori(0, (TURNS - 1) // 2) as i:
                step.at = i * 2
                gathers(i * 2 + 1, 1)
                gathers(i * 2 + 2, 0)
            assert TURNS % 2 == 1

        @block.tensor
        def _(pe):
            pe.wait_ge(consts, 2)
            pe.wait_ge(ld_w, 16 * (1 + 2 * HEADS + 8))
            nc.tensor.transpose(acc[0][:, 0:F], w0s[:, :], ident[:, :]).then_inc(prep_in, 1)
            pe.wait_ge(prep_out, 1)
            nc.tensor.matmul(acc[1][:, 0:2 * HEADS], w0T[:, :], ablk[:, :], start=True, stop=True).then_inc(prep_in, 1)
            pe.wait_ge(ld_w2, 16 * 16)
            nc.tensor.transpose(acc[2][:, 0:F], wnT[:, :], ident[:, :]).then_inc(prep_in, 1)
            nc.tensor.transpose(acc[3][:, 0:F], wsT[:, :], ident[:, :]).then_inc(prep_in, 1)
            pe.wait_ge(prep_out, 4)
            pe.wait_ge(ld_x, 32)

            def turn_x(q, first):
                if q == 8:
                    pe.wait_ge(xT_ready, first + 1)
                for t in range(q * BT, min(NT, q * BT + BT)):
                    last = nc.tensor.transpose(acc[q % 8][:, (t % BT) * TS:(t % BT + 1) * TS], xs[0:TS, t, :], ident[0:TS, 0:TS])
                last.then_inc(xT_in, 1)

            for q in range(NB):
                turn_x(q, 0)
            pe.wait_ge(xT_ready, NB)
            for t in range(NT):
                if t >= 4:
                    pe.wait_ge(prep_out, 4 + t - 3)
                nc.tensor.matmul(acc[t % 4][0:TS, 0:F + 2 * HEADS], xT[:, t * TS:(t + 1) * TS], wcat[:, :],
                                 start=True, stop=True).then_inc(prep_in, 1)
            pe.wait_ge(totals_ready, 1)
            nc.tensor.matmul(acc[4][0:EP, 0:NBIN], tril[0:EP, 0:EP], bins[0:EP, 0, :], start=True, stop=True)
            nc.tensor.matmul(acc[4][:, 128:128 + NBIN], ones[0:EP, :], bins[0:EP, 0, :], start=True, stop=True).then_inc(prefix_in, 1)

            def edge_logits(i):
                pe.wait_ge(ein_ready, i + 1)
                for k in range(4):
                    last = nc.tensor.transpose(acc[5][:, k * EP:(k + 1) * EP], ein[:, k * 128:(k + 1) * 128], ident[0:EP, 0:EP])
                last.then_inc(eT_in, 1)
                pe.wait_ge(eT_out, i + 1)
                for k in range(4):
                    last = nc.tensor.matmul(acc[6][0:EP, k * 32:(k + 1) * 32], eT[:, k * EP:(k + 1) * EP], edgeblk[:, :],
                                            start=True, stop=True)
                last.then_inc(el_in, 1)

            with pe.Fori(0, EC // 32) as i:
                edge_logits(i)

            pe.wait_ge(lut_in, 1)
            for k in range(12):
                last = nc.tensor.transpose(acc[k // 6][0:NT, :].bitcast(BF16)[:, (k % 6) * TS:(k % 6 + 1) * TS],
                                           s3[:, :, :, :].rearrange("p t h k -> p t (h k)")[:, :, k], identb[0:TS, 0:TS])
            last.then_inc(lut_pe, 1)
            pe.wait_ge(lut_act, 1)
            for k in range(24):
                if k >= 4:
                    pe.wait_ge(lut_act, k - 2)
                nc.tensor.matmul(acc[k % 4][0:TS, 0:NC // 2], s3T[:, k // 2, :], inTile[:, (k % 2) * (NC // 2):(k % 2 + 1) * (NC // 2)],
                                 start=True, stop=True).then_inc(lut_pe, 1)
            pe.wait_ge(lut_act, 25)
            pe.wait_ge(el_out, EC // 32)
            pe.wait_ge(prep_out, 4 + NT)
            pe.wait_ge(offs_read, 1)
            pe.wait_ge(zero_ready, 1)
            for b in range(7):
                last = nc.tensor.matmul(acc[b][:, :], zerob[:, :], zerow[:, :].bitcast(BF16)[:, 0:BANK], start=True, stop=False, skip_group_check=True)

            def turn_stat(i, k):
                pe.wait_ge(stat_ready, i * UN + k + 1)
                if not (isinstance(i, int) and i * UN + k == 0):
                    pe.wait_ge(looked, i * UN + k)
                for j in range(GR):
                    last = nc.tensor.transpose(psT[:, j, :], stat[:, (k % UN) * GR + j, 0:TS], identb[:, :])
                last.then_inc(turned, 1)

            def look_up(i, k):
                pe.wait_ge(dT_ready, i * UN + k + 1)
                for j in range(GR):
                    c = (i * UN + k) * GR + j
                    last = nc.tensor.matmul(psS[:, j * 12:(j + 1) * 12], dT[:, (k % UN) * GR + j, :],
                                            lut[:, ds(c, 1), :].rearrange("p c h -> p (c h)"), start=True, stop=True)
                last.then_inc(src_logits, 1)

            def products(i, k, j, high):
                s = (k % UN) * GR + j
                pe.wait_ge(hot_ready, (i * UN + k) * GR + (j + 1))
                for b, (at, n) in enumerate(DB[HB:] if high else DB[:HB]):
                    nc.tensor.matmul(acc[b + HB * high][:, 0:n], stat[:, s, :], hot[k % 2 * GR + j][:, b * BANK:b * BANK + n],
                                     start=False, stop=False, skip_group_check=True)
                nc.tensor.matmul(acc[6][0:TS, HCOL:HCOL + F], statf[:, s, :], msg[:, s, :],
                                 start=False, stop=False, skip_group_check=True).then_inc(main_done, 1)

            def group(i, k, ahead, chunk):
                for j in range(GR):
                    chunk(j)
                    if ahead and j == 0:
                        turn_stat(i, k + 2)
                    if ahead and j == 1:
                        look_up(i, k + 2)

            def turn(i, last=False):
                for k in range(UN):
                    ahead = not (last and k + 2 >= UN)
                    pe.wait_ge(msg_ready, i * UN + k + 1)
                    pe.wait_ge(statf_ready, i * UN + k + 1)
                    code, ends = load_codes(pe, i, k)
                    with pe.If(ends % (1 << (GR - 1)) != 0):
                        def chunk(j):
                            own = code_of(code, ends, j)
                            pe.wait_ge(released, own)
                            with pe.If(own % 2 == 1):
                                products(i, k, j, 0)
                            with pe.Else():
                                products(i, k, j, 1)
                        group(i, k, ahead, chunk)
                    with pe.Else():
                        pe.wait_ge(released, code)
                        with pe.If(code % 2 == 1):
                            group(i, k, ahead, lambda j: products(i, k, j, 0))
                        with pe.Else():
                            group(i, k, ahead, lambda j: products(i, k, j, 1))

            for k in range(2):
                turn_stat(0, k)
                look_up(0, k)
            turn(0)
            with pe.Fori(1, TURNS - 1) as i:
                turn(i)
            turn(TURNS - 1, last=True)

            for lay in range(3):
                pe.wait_ge(x_ready, lay + 1)
                pe.wait_ge(esum_ready, 2)
                if lay:
                    pe.wait_ge(blk_used, NB * lay)
                if lay < 2:
                    for q in range(NB):
                        turn_x(q, NB * (lay + 1))
                    pe.wait_ge(xT_ready, NB * (lay + 2))
                if lay == 0:
                    for b, (at, n) in enumerate(DB):
                        last = nc.tensor.matmul(acc[b][:, 0:n], degsel[TS:128, :], esum[TS:128, at:at + n], start=True, stop=True)
                    last.then_inc(deg_in, 1)
                    pe.wait_ge(deg_out, 1)
                pe.wait_ge(halves_ready, lay + 1)

                def count_tile(k, tile, start):
                    for h, half in enumerate((xh, xl)):
                        for b, (at, n) in enumerate(DB):
                            last = nc.tensor.matmul(acc[b][:, 0:n], half[:, ds(k, 1), :].rearrange("p t f -> p (t f)"),
                                                    tile[:, at:at + n], start=start and h == 0, stop=False,
                                                    skip_group_check=True)
                    last.then_inc(tile_used, 1)

                pe.wait_ge(count_in[AR], 16 * (lay + 1))
                count_tile(0, ring0, True)
                with pe.Fori(0, (NT - 1) // AR) as i:
                    for s in range(AR):
                        pe.wait_ge(count_in[s], i * 16 + 16 * (lay * ((NT - 1) // AR) + 1))
                        count_tile(i * AR + (1 + s), ring[:, s, :], False)
                pe.wait_ge(neigh_out, 7 * (lay + 1))
                for q in range(NB):
                    tiles = range(q * BT, min(NT, q * BT + BT))
                    n = len(tiles) * TS
                    cols = slice(q * BW, q * BW + n)
                    if lay == 1:
                        at = 9 * q
                        nc.tensor.matmul(acc[7][:, 0:n], wgs[:, 0, :], neT[:, cols], start=True, stop=False)
                        nc.tensor.matmul(acc[7][:, 0:n], wgs[:, 1, :], xT[:, cols], start=False, stop=True).then_inc(mlp_in, 1)
                        pe.wait_ge(mlp_out, at + 1)
                        if q == 0:
                            pe.wait_ge(ld_w3, 48)
                        if q:
                            pe.wait_ge(blk_used, NB + q)
                        for m in range(KH):
                            nc.tensor.matmul(acc[m][:, 0:n], w1s[:, m * F:(m + 1) * F], h0[:, 0:n], start=True, stop=True).then_inc(mlp_in, 1)
                        pe.wait_ge(mlp_out, at + 5)
                        for m in range(KH):
                            for k in range(KH):
                                last = nc.tensor.matmul(acc[4 + m][:, 0:n], w2s[:, k, m * F:(m + 1) * F], h1[:, k, 0:n],
                                                        start=k == 0, stop=k == KH - 1)
                            last.then_inc(mlp_in, 1)
                        pe.wait_ge(mlp_out, at + 9)
                        bank = 0
                    else:
                        bank = q % 8
                        if q == 8:
                            pe.wait_ge(blk_used, NB * lay + 1)
                    for j, t in enumerate(tiles):
                        to = acc[bank][0:TS, j * F:(j + 1) * F]
                        tc_ = slice(t * TS, (t + 1) * TS)
                        if lay == 0:
                            nc.tensor.matmul(to, neT[:, tc_], wnT[:, :], start=True, stop=False)
                            nc.tensor.matmul(to, xT[:, tc_], wsT[:, :], start=False, stop=False)
                            last = nc.tensor.matmul(to, ones[0:2, 0:TS], brow1[:, :], start=False, stop=True)
                        elif lay == 1:
                            for k in range(KH):
                                nc.tensor.matmul(to, h2[:, k, j * TS:(j + 1) * TS], w3s[:, k, :], start=k == 0, stop=False)
                            last = nc.tensor.matmul(to, ones[0:1, 0:TS], brow3[:, :], start=False, stop=True)
                        else:
                            nc.tensor.matmul(to, neT[:, tc_], w4s[:, :], start=True, stop=False)
                            last = nc.tensor.matmul(to, esum[TS:128, tc_], wext[TS:128, :], start=False, stop=True)
                    last.then_inc(blk_ready, 1)

        @block.scalar
        def _(act):
            act.wait_ge(prep_in, 1)
            nc.scalar.copy(w0T[:, :], acc[0][:, 0:F]).then_inc(prep_out, 1)
            act.wait_ge(prep_in, 2)
            nc.scalar.copy(wcat[:, 0:F], w0s[:, :])
            nc.scalar.copy(wcat[:, F:F + 2 * HEADS], acc[1][:, 0:2 * HEADS]).then_inc(prep_out, 1)
            act.wait_ge(prep_in, 4)
            nc.scalar.copy(wnT[:, :], acc[2][:, 0:F]).then_inc(prep_out, 1)
            nc.scalar.copy(wsT[:, :], acc[3][:, 0:F]).then_inc(prep_out, 1)

            def copy_xT(first):
                for q in range(NB):
                    n = min(NPAD - q * BW, BW)
                    act.wait_ge(xT_in, first + q + 1)
                    nc.scalar.copy(xT[:, q * BW:q * BW + n], acc[q % 8][:, 0:n]).then_inc(xT_ready, 1)

            copy_xT(0)
            for t in range(NT):
                if t and t % TT == 0:
                    act.wait_ge(piece_done, 16 * (t // TT))
                act.wait_ge(prep_in, 4 + t + 1)
                ins = nc.scalar.copy(tpiece[:, t % TT, :], acc[t % 4][0:TS, 0:TW])
                if t % TT == TT - 1:
                    ins.then_inc(piece_ready, 1)
                nc.scalar.copy(ssrc[:, t, :], acc[t % 4][0:TS, TW:TW + HEADS]).then_inc(prep_out, 1)

            act.wait_ge(ld_e16, 32)

            def edge_logits(i):
                nc.scalar.copy(ein[:, :], ea16s[:, ds(i * 512, 512)]).then_inc(ein_ready, 1)
                act.wait_ge(eT_in, i + 1)
                nc.scalar.copy(eT[:, :], acc[5][:, 0:4 * EP]).then_inc(eT_out, 1)
                act.wait_ge(el_in, i + 1)
                nc.scalar.copy(rec[:, ds(i * 32, 32), R_EA:R_EA + HEADS],
                               acc[6][0:EP, 0:128].rearrange("p (c h) -> p c h", h=HEADS)).then_inc(el_out, 1)

            with act.Fori(0, EC // 32) as i:
                edge_logits(i)

            def exp_group(i, k):
                act.wait_ge(shifted, i * UN + k + 1)
                nc.scalar.activation(smalls[:, k % 2, 16:32], smalls[:, k % 2, 0:16], ACT.Exp).then_inc(exped, 1)

            def copy_stat(i, k):
                act.wait_ge(turned, i * UN + k + 1)
                s = (k % UN) * GR
                nc.scalar.copy(dT[:, s:s + GR, :], psT[:, :, :]).then_inc(dT_ready, 1)
                if not (isinstance(i, int) and i * UN + k < UN):
                    act.wait_ge(main_done, (i * UN + k) * GR - (UN - 1) * GR)
                nc.scalar.copy(statf[:, s:s + GR, :], stat[:, s:s + GR, 0:TS]).then_inc(statf_ready, 1)

            def evacuate(code, high):
                banks = list(enumerate(DB))[HB:2 * HB] if high else list(enumerate(DB))[:HB]
                for b, (at, n) in banks:
                    last = nc.scalar.copy(stage[:, at:at + n], acc[b][0:TS, 0:n])
                last.then_inc(copied, 1)
                act.wait_ge(copied, code)
                for b, (at, n) in banks:
                    last = nc.scalar.copy(acc[b][0:TS, 0:n], zerow[0:TS, 0:n])
                last.then_inc(half_out[high], 1)

            def chunk_end(i, k, j, code):
                c = (i * UN + k) * GR + j
                order = nc.s_assert_within((code + 1) // 2, 1, NT,
                                           skip_runtime_bounds_check_because="only real bins have ends, and there are 2 NT")
                act.wait_ge(main_done, c + 1)
                with act.If(code % 2 == 1):
                    act.wait_ge(half_free[0], order)
                    evacuate(code, 0)
                with act.Else():
                    act.wait_ge(half_free[1], order)
                    nc.scalar.copy(stage[:, 2 * LOW:DW], acc[6][0:TS, 0:DW - 2 * LOW])
                    nc.scalar.copy(ys[0:TS, ds(order - 1, 1), :].rearrange("p t f -> p (t f)"), acc[6][0:TS, HCOL:HCOL + F]).then_inc(six_out, 1)
                    act.wait_ge(six_out, order)
                    nc.scalar.copy(acc[6][0:TS, 0:HCOL + F], zerow[0:TS, 0:HCOL + F]).then_inc(six_zero, 1)
                    act.wait_ge(six_zero, order)
                    act.wait_ge(half_out[0], order)
                    act.sem_inc(released, 1)
                    evacuate(code, 1)
                    act.wait_ge(half_out[1], order)
                    act.sem_inc(released, 1)

            def turn(i, last=False):
                for k in range(UN):
                    code, ends = load_codes(act, i, k)
                    if not (last and k + 1 >= UN):
                        exp_group(i, k + 1)
                    if not (last and k + 2 >= UN):
                        copy_stat(i, k + 2)
                    with act.If(ends != 0):
                        for j in range(GR):
                            with act.If(bit(ends, j) == 1):
                                chunk_end(i, k, j, code_of(code, ends, j))

            act.wait_ge(lut_pe, 1)
            for k in range(2):
                last = nc.scalar.copy(s3T[:, k * 6:k * 6 + 6, :], acc[k][0:NT, :].bitcast(BF16)[:, 0:6 * TS].rearrange("p (k s) -> p k s", k=6))
            last.then_inc(lut_act, 1)
            for k in range(24):
                act.wait_ge(lut_pe, k + 2)
                last = nc.scalar.copy(lut[:, (k % 2) * (NC // 2):(k % 2 + 1) * (NC // 2), k // 2], acc[k % 4][0:TS, 0:NC // 2])
                last.then_inc(lut_act, 1)
            act.wait_ge(lut_act, 25)
            act.sem_inc(lut_in, 1)
            act.wait_ge(maps_ready, 1)
            act.sem_inc(released, 2)
            copy_stat(0, 0)
            exp_group(0, 0)
            copy_stat(0, 1)
            turn(0)
            with act.Fori(1, TURNS - 1) as i:
                turn(i)
            turn(TURNS - 1, last=True)
            act.wait_ge(main_done, NC)
            for b, (at, n) in enumerate(DB):
                last = nc.scalar.copy(esum[TS:128, at:at + n], acc[b][TS:128, 0:n])
            last.then_inc(esum_ready, 1)

            act.wait_ge(elu_in, 1)
            nc.scalar.activation(scr, scr, ACT.Exp).then_inc(elu_exp, 1)
            for lay in range(4):
                act.wait_ge(root_in, lay + 1)
                nc.scalar.activation(st[0:TS, 1, :], st[0:TS, 0, :], ACT.Sqrt).then_inc(root_out, 1)
                if lay == 3:
                    break
                act.wait_ge(x_ready, lay + 1)
                nc.scalar.mul(xh, xr, XS).then_inc(xh_ready, 1)
                if lay < 2:
                    copy_xT(NB * (lay + 1))
                if lay != 1:
                    act.wait_ge(tile_used, NT * (lay + 1))
                    for b, (at, n) in enumerate(DB):
                        nc.scalar.mul(neT[:, at:at + n], acc[b][:, 0:n], 1.0 / XS).then_inc(neigh_out, 1)
                else:
                    for q in range(NB):
                        n = min(NPAD - q * BW, BW)
                        at = 9 * q
                        act.wait_ge(mlp_in, at + 1)
                        nc.scalar.activation(h0[:, 0:n], acc[7][:, 0:n], ACT.Relu, bias=bcol[:, 0:1]).then_inc(mlp_out, 1)
                        for m in range(KH):
                            act.wait_ge(mlp_in, at + 2 + m)
                            nc.scalar.activation(h1[:, m, 0:n], acc[m][:, 0:n], ACT.Tanh, bias=bcol[:, 1 + m:2 + m]).then_inc(mlp_out, 1)
                        for m in range(KH):
                            act.wait_ge(mlp_in, at + 6 + m)
                            nc.scalar.activation(h2[:, m, 0:n], acc[4 + m][:, 0:n], ACT.Tanh, bias=bcol[:, 1 + KH + m:2 + KH + m]).then_inc(mlp_out, 1)

        @block.vector
        def _(dve):
            step = Steps(dve, dve_step)
            V = nc.vector
            dve.wait_ge(ld_ends, 64)
            step.done(V.tensor_copy(rec[:, :, R_DST].bitcast(I32), dsti))
            step.done(V.tensor_copy(work, srci))
            step.done(V.tensor_scalar(pos, dsti, float(LOW), -float(LOW), ALU.is_ge, ALU.mult))
            step(V.tensor_scalar(posi, srci, 5, None, ALU.logical_shift_right))
            step.done(V.tensor_tensor(rec[:, :, R_DC], pos, dsti, ALU.add))
            step(V.tensor_scalar(tidf, posi, 1.0 / 3, -1.0 / 3, ALU.mult, ALU.add))
            step(V.tensor_scalar(tidf, tidf, RNE, None, ALU.add))
            step(V.tensor_scalar(tidf, tidf, -RNE, None, ALU.add))
            step(V.scalar_tensor_tensor(rec[:, :, R_SL], tidf, float(-TS), work, ALU.mult, ALU.add))
            step.done(V.tensor_scalar(half, pos, -1023.0 / LOW, 1.0, ALU.mult, ALU.add))
            step(V.tensor_scalar(work, pos, -0.5 / LOW, None, ALU.mult))
            step.done(V.tensor_tensor(work, work, tidf, ALU.add))
            dve.wait_ge(consts, 2)
            step.wait()
            for t in range(NT):
                step(V.scalar_tensor_tensor(pos, tidf, binid[0:EP, t:t + 1], half, ALU.is_equal, ALU.mult,
                                            accum_out=bins[0:EP, 1, t:t + 1]))
            step(V.tensor_copy(binsi[0:EP, 0:NT], bins[0:EP, 1, 0:NT]))
            step.done(V.tensor_scalar(binsi[0:EP, NT:NBIN], binsi[0:EP, 0:NT], 10, None, ALU.logical_shift_right))
            step.done(V.tensor_scalar(binb, work, 2.0, None, ALU.mult))
            step(V.tensor_scalar(binsi[0:EP, 0:NT], binsi[0:EP, 0:NT], 1023, None, ALU.bitwise_and))
            step.done(V.memset(zero, 0.0))
            V.tensor_copy(bins[0:EP, 0, :].rearrange("p (t h) -> p h t", h=2),
                          binsi[0:EP, :].rearrange("p (h t) -> p h t", h=2)).then_inc(totals_ready, 1)
            dve.wait_ge(totals_ready, 1)
            step.wait()
            dve.wait_ge(prefix_in, 1)
            step(V.tensor_scalar(bins[:, 2, :], acc[4][:, 128:128 + NBIN], float(CH - 1), None, ALU.add))
            step(V.tensor_copy(binsi[:, :], bins[:, 2, :]))
            step(V.tensor_scalar(binsi[:, :], binsi[:, :], 7, None, ALU.logical_shift_right))
            step.done(V.memset(bins[:, 5, :], 0.0))
            step(V.tensor_copy(bins[:, 3, :], binsi[:, :]))
            step(V.tensor_scalar(bins[:, 3, :], bins[:, 3, :], 1.0, None, ALU.max))
            step(V.tensor_tensor_scan(bins[:, 4, :], bins[:, 3, :], bins[:, 5, :], 0.0, ALU.add, ALU.add))
            step(V.tensor_tensor(bins[:, 2, :], bins[:, 4, :], bins[:, 3, :], ALU.subtract))
            step(V.tensor_scalar(bins[:, 2, :], bins[:, 2, :], float(CH), -1.0, ALU.mult, ALU.add))
            V.tensor_tensor(carry[:, :], bins[0:EP, 2, :], acc[4][0:EP, 0:NBIN], ALU.add).then_inc(offs_read, 1)
            dve.wait_ge(offs_read, 1)
            start = 0
            for cols in BLOCKS:
                at = slice(start, start + cols)
                for b in range(0, NBIN, 2):
                    for u in range(2):
                        step.done(V.tensor_scalar(masks[u].bitcast(BF16)[:, 0:cols], binb[:, at], binid[0:EP, b + u:b + u + 1], None, ALU.is_equal))
                    step.wait()
                    for u in range(2):
                        step.done(V.tensor_tensor_scan(cums[u][:, 0:cols], masks[u].bitcast(BF16)[:, 0:cols], zero[:, 0:cols],
                                                       carry[:, b + u:b + u + 1], ALU.add, ALU.add))
                    step.wait()
                    for u in range(2):
                        step.done(V.tensor_copy(carry[:, b + u:b + u + 1], cums[u][:, cols - 1:cols]))
                        step(V.copy_predicated(pos[:, at], masks[u].bitcast(mybir.dt.int16)[:, 0:cols], cums[u][:, 0:cols]))
                step(V.tensor_copy(posi[:, at], pos[:, at]))
                step.done(V.tensor_scalar(whole[0][:, 0:cols], posi[:, at], CH - 1, None, ALU.bitwise_and))
                step(V.tensor_scalar(whole[1][:, 0:cols], posi[:, at], 7, None, ALU.logical_shift_right))
                step.done(V.tensor_copy(cums[0][:, 0:cols], whole[0][:, 0:cols]))
                step(V.tensor_copy(cums[1][:, 0:cols], whole[1][:, 0:cols]))
                step(V.scalar_tensor_tensor(pos[:, at], cums[0][:, 0:cols], float(NC), cums[1][:, 0:cols], ALU.mult, ALU.add))
                V.tensor_copy(posi[:, at], pos[:, at]).then_inc(ranked, 1)
                start += cols
            dve.wait_ge(ranked, len(BLOCKS))
            dve.wait_ge(prep_out, 4 + NT)
            for part in range(3):
                step(V.tensor_copy(s3[:, :, :, part], ssrc[:, :, :]))
                if part < 2:
                    step(V.tensor_tensor(ssrc[:, :, :], ssrc[:, :, :], s3[:, :, :, part], ALU.subtract))
            step(V.memset(mf[0:1, 0, :], 0.0))
            dve.wait_ge(chunk_ids, 1)
            for k in range(2):
                if k:
                    step(V.tensor_copy(beside, bins[0:NT, 4, 1:NBIN:2]))
                    step(V.memset(beside[:, NT - 1:NT], FAR))
                else:
                    step(V.tensor_tensor(beside, bins[0:NT, 4, 0:NBIN:2], bins[0:NT, 3, 0:NBIN:2], ALU.subtract))
                step(V.tensor_tensor(bins[0:NT, 2, 0:NT], beside, ident[0:NT, 0:NT], ALU.mult))
                step(V.tensor_reduce(endc[:, k:k + 1], bins[0:NT, 2, 0:NT], AX, ALU.add))
            step(V.tensor_scalar(mf[:, 2, 0:NC], mf[:, 1, 0:NC], endc[:, 0:1], None, ALU.is_ge))
            dve.wait_ge(el_out, EC // 32)
            V.scalar_tensor_tensor(inTile, mf[:, 1, 0:NC], endc[:, 1:2], mf[:, 2, 0:NC], ALU.is_lt, ALU.mult).then_inc(lut_in, 1)
            for b in range(NBIN):
                step(V.scalar_tensor_tensor(mf[0:1, 0, :], mf[0:1, 1, :], bins[0:1, 4, b:b + 1], mf[0:1, 0, :], ALU.is_ge, ALU.add))
            m4 = mf[0:1, 0, 0:NC].rearrange("p (g j) -> p g j", j=GR)
            e4 = mf[0:1, 0, 1:NC + 1].rearrange("p (g j) -> p g j", j=GR)
            n4 = mf[0:1, 2, 0:NC].rearrange("p (g j) -> p g j", j=GR)
            step(V.tensor_tensor(n4, e4, m4, ALU.subtract))
            for j in range(1, GR):
                step(V.scalar_tensor_tensor(n4[:, :, 0:1], n4[:, :, j:j + 1], float(1 << j), n4[:, :, 0:1], ALU.mult, ALU.add))
            step(V.scalar_tensor_tensor(n4[:, :, 0:1], m4[:, :, 0:1], float(1 << GR), n4[:, :, 0:1], ALU.mult, ALU.add))
            step(V.tensor_scalar(tmap[:, :].rearrange("p (g j) -> p g j", j=1), n4[:, :, 0:1], float(1 << GR), None, ALU.add))
            dve.wait_ge(lut_in, 2)
            step(V.memset(stat[:, :, :], 0.0))
            V.memset(stat[:, :, OCOL:OCOL + 2], 1.0).then_inc(maps_ready, 1)
            dve.wait_ge(maps_ready, 1)
            dve.wait_ge(consts, 3)
            dve.wait_ge(recs_in, 16)
            V.memset(zerow[:, :], 0.0).then_inc(zero_ready, 1)

            def stat_tiles(i, k):
                s = (k % UN) * GR
                if not (isinstance(i, int) and i * UN + k < UN):
                    dve.wait_ge(main_done, (i * UN + k) * GR - (UN - 1) * GR)
                V.tensor_tensor(stat[:, s:s + GR, 0:TS],
                                iotas[:, :].rearrange("p (a f) -> p a f", a=1).to_broadcast([128, GR, TS]),
                                recs[:, ds((i * UN + k) * GR, GR), R_SL:R_SL + 1].to_broadcast([128, GR, TS]), ALU.is_equal)

            def stat_features(i, k):
                s = (k % UN) * GR
                V.tensor_copy(stat[:, s:s + GR, TS:OCOL],
                              recsb[:, ds((i * UN + k) * GR, GR), 2 * R_E6:2 * R_E6 + E6C]).then_inc(stat_ready, 1)

            def one_hot(i, k, j):
                c = (i * UN + k) * GR + j
                if not (isinstance(i, int) and c < 2 * GR):
                    dve.wait_ge(main_done, c - (2 * GR - 1))
                V.tensor_scalar(hot[k % 2 * GR + j], iotad[:, :], recs[:, ds(c, 1), R_DC:R_DC + 1].rearrange("p c w -> p (c w)"),
                                None, ALU.is_equal).then_inc(hot_ready, 1)

            PER_TURN = 7 * UN

            def attention(i, k, hots=False, stats=False):
                s = (k % UN) * GR
                z, e = smalls[:, k % 2, 0:16], smalls[:, k % 2, 16:32]
                m, n = smalls[:, k % 2, 32:36], smalls[:, k % 2, 36:40]
                z3, e3 = z.rearrange("p (j h) -> p j h", h=HEADS), e.rearrange("p (j h) -> p j h", h=HEADS)
                over = [v.rearrange("p (j a) -> p j a", a=1).to_broadcast([128, GR, HEADS]) for v in (m, n)]
                dve.wait_ge(src_logits, i * UN + k + 1)
                V.tensor_reduce(z, psS[:, :].rearrange("p (a b) -> p a b", b=3), AX, ALU.add).then_inc(looked, 1)
                if hots:
                    one_hot(i, k - 1, 0)
                dve.wait_ge(looked, i * UN + k + 1)
                step.done(V.tensor_tensor(z3, z3, recs[:, ds((i * UN + k) * GR, GR), R_EA:R_EA + HEADS], ALU.add))
                if hots:
                    one_hot(i, k - 1, 1)
                step.wait()
                for j in range(GR):
                    dve.wait_ge(gathered[s + j], (i + k // UN) * 16 + 16)
                step.done(V.tensor_tensor(z3, z3, gt[:, s:s + GR, F:TW], ALU.add))
                if stats:
                    stat_tiles(i, k + 2)
                step.wait()
                step.done(V.scalar_tensor_tensor(z, z, ALPHA, z, ALU.mult, ALU.max))
                if stats:
                    stat_features(i, k + 2)
                step.wait()
                step(V.tensor_reduce(m, z3, AX, ALU.max))
                V.tensor_tensor(z3, z3, over[0], ALU.subtract).then_inc(shifted, 1)
                if hots:
                    one_hot(i, k - 1, 2)
                dve.wait_ge(exped, i * UN + k + 1)
                step.done(V.tensor_reduce(n, e3, AX, ALU.add))
                if hots:
                    one_hot(i, k - 1, 3)
                step.wait()
                step(V.reciprocal(n, n))
                step(V.tensor_tensor(e3, e3, over[1], ALU.mult))
                if not (isinstance(i, int) and i * UN + k < UN):
                    dve.wait_ge(main_done, (i * UN + k) * GR - (UN - 1) * GR)
                to = msg[:, s:s + GR, :].rearrange("p j (h d) -> p j h d", h=HEADS)
                frm = gt[:, s:s + GR, 0:F].rearrange("p j (h d) -> p j h d", h=HEADS)
                at4 = e3.rearrange("p j (h a) -> p j h a", a=1).to_broadcast([128, GR, HEADS, HF])
                V.tensor_tensor(to, frm, at4, ALU.mult).then_inc(msg_ready, 1)

            def turn(i, last=False):
                for k in range(UN):
                    if last and k + 1 >= UN:
                        for j in range(GR):
                            one_hot(i, k, j)
                    else:
                        attention(i, k + 1, hots=True, stats=not (last and k + 3 >= UN))

            for k in range(3):
                stat_tiles(0, k)
                stat_features(0, k)
            attention(0, 0)
            turn(0)
            before = step.n
            with dve.Fori(1, TURNS - 1) as i:
                step.at = i * PER_TURN - PER_TURN
                turn(i)
                assert step.n == before + PER_TURN
            step.at = 0
            step.n = before + PER_TURN * (TURNS - 2)
            turn(TURNS - 1, last=True)

            for h in range(2):
                dve.wait_ge(half_out[h], NT)
            dve.wait_ge(esum_ready, 1)
            step.done(V.memset(neT[:, DW:NPAD], 0.0))
            V.memset(esum[:, DW:NPAD], 0.0).then_inc(esum_ready, 1)
            V.tensor_scalar(scr, yr, 0.0, None, ALU.min).then_inc(elu_in, 1)
            dve.wait_ge(elu_in, 1)
            step(V.scalar_tensor_tensor(yr, yr, 0.0, xr, ALU.max, ALU.add))
            dve.wait_ge(elu_exp, 1)
            step(V.scalar_tensor_tensor(yr, scr, -1.0, yr, ALU.add, ALU.add))

            def wide(v):
                return v.rearrange("p (t a) -> p t a", a=1).to_broadcast([TS, NT, F])

            def norm():
                step(V.tensor_reduce(st[0:TS, 0, :], yr, AX, ALU.add))
                step(V.tensor_scalar(st[0:TS, 0, :], st[0:TS, 0, :], -1.0 / F, None, ALU.mult))
                step(V.tensor_tensor(xr, yr, wide(st[0:TS, 0, :]), ALU.add))
                step(V.tensor_tensor(yr, xr, xr, ALU.mult))
                step(V.tensor_reduce(st[0:TS, 0, :], yr, AX, ALU.add))
                V.tensor_scalar(st[0:TS, 0, :], st[0:TS, 0, :], 1.0 / F, EPS, ALU.mult, ALU.add).then_inc(root_in, 1)

            for lay in range(4):
                norm()
                dve.wait_ge(root_out, lay + 1)
                step(V.reciprocal(st[0:TS, 2, :], st[0:TS, 1, :]))
                V.tensor_tensor(xr, xr, wide(st[0:TS, 2, :]), ALU.mult).then_inc(x_ready, 1)
                if lay == 3:
                    break
                dve.wait_ge(x_ready, lay + 1)
                dve.wait_ge(xh_ready, lay + 1)
                V.scalar_tensor_tensor(xl, xr, XS, xh, ALU.mult, ALU.subtract).then_inc(halves_ready, 1)
                if lay == 0:
                    dve.wait_ge(deg_in, 1)
                    for b, (at, n) in enumerate(DB):
                        last = V.tensor_scalar(rdeg[:, at:at + n], acc[b][:, 0:n], 1.0, None, ALU.max)
                    last.then_inc(deg_out, 1)
                    dve.wait_ge(deg_out, 1)
                    step(V.reciprocal(rdeg[:, 0:DW], rdeg[:, 0:DW]))
                if lay == 1:
                    dve.wait_ge(tile_used, NT * 2)
                    for b, (at, n) in enumerate(DB):
                        V.scalar_tensor_tensor(neT[:, at:at + n], acc[b][:, 0:n], 1.0 / XS, rdeg[:, at:at + n],
                                               ALU.mult, ALU.mult).then_inc(neigh_out, 1)
                for q in range(NB):
                    n = min(NT - q * BT, BT)
                    dve.wait_ge(blk_ready, NB * lay + q + 1)
                    ps = acc[0 if lay == 1 else q % 8][0:TS, 0:n * F]
                    yb, xb = (v[0:TS, q * BT:q * BT + n, :].rearrange("p t f -> p (t f)") for v in (ys, xs))
                    if lay < 2:
                        V.tensor_tensor(yb, ps, xb, ALU.add).then_inc(blk_used, 1)
                    else:
                        V.scalar_tensor_tensor(yb, ps, 0.0, xb, ALU.max, ALU.add).then_inc(blk_used, 1)
                dve.wait_ge(blk_used, NB * (lay + 1))
    return nc


_INS = ['x', 'src', 'dst', 'edge_attr_16', 'edge_attr_6', 'L0_gnn_W', 'L0_gnn_a', 'L1_gnn_W_neigh', 'L1_gnn_b_neigh',
        'L1_gnn_W_self', 'L1_gnn_b_self', 'L2_gnn_Wg', 'L2_gnn_Ws', 'L2_gnn_bg', 'L2_gnn_W1', 'L2_gnn_b1', 'L2_gnn_W2',
        'L2_gnn_b2', 'L2_gnn_W3', 'L2_gnn_b3', 'L3_gnn_W', 'L3_gnn_b', 'L3_gnn_We', 'L3_gnn_be']


def kernel(**inputs):
    import numpy as _np
    import concourse.bacc as _bacc
    from concourse import mybir as _mybir
    from concourse.bass_utils import run_bass_kernel_spmd as _run

    nc = _bacc.Bacc("TRN2", target_bir_lowering=False, num_devices=1)
    arrays, args = {}, []
    for name in _INS:
        a = _np.ascontiguousarray(inputs[name])
        arrays[f"in_{name}"] = a
        args.append(nc.dram_tensor(f"in_{name}", a.shape, _mybir.dt.from_np(a.dtype), kind="ExternalInput").ap())
    args.append(nc.dram_tensor("out", (N, F), FP32, kind="ExternalOutput").ap())
    gnn_stack(nc, *args)
    r = _run(nc, [arrays], core_ids=[0])
    return r.results[0]["out"]
```

```python
import concourse.bass as bass
from concourse import mybir
from contextlib import ExitStack

FP32 = mybir.dt.float32
BF16 = mybir.dt.bfloat16
FP16 = mybir.dt.float16
I32 = mybir.dt.int32
ALU = mybir.AluOpType
ACT = mybir.ActivationFunctionType
AX = mybir.AxisListType.X
ds = bass.ds

N = 3125
E = 100000
F = 128
HEADS, HF = 4, 32
EF0, EF3 = 16, 6
HID = 512
KH = HID // F
MLP_ORDER = [1, 2, 3, 0]

TS = 96
NT = -(-N // TS)
LAST = N - TS * (NT - 1)
NPAD = NT * TS
EP, EC = 125, 800
CH = 128
GR = 4
UN = 8
RG = 4
NBIN = 2 * NT
NC = -(-(E // CH + NBIN) // (GR * RG)) * GR * RG
NG = NC // GR
TURNS = -(-NG // UN)
FIRST = 2 * GR * UN
SLOTS = GR * RG
BANK = 512
DW = 3136
DB = [(b * BANK, min(BANK, DW - b * BANK)) for b in range(-(-DW // BANK))]
HB = 3
LOW = HB * BANK
HW_ = DW - LOW
BLOCKS = [64, 96, 160, 224, 256]
HALF = 16
W = 16
R_DST, R_DC, R_SL, R_EA, R_E6 = 0, 1, 2, 3, 7
TW = F + HEADS
E6C = 3 * EF3
OCOL = TS + E6C
HCOL = 64
FAR = 20000.0
CS = 1.0 / 16
XS = 4096.0
ALPHA = 0.2
EPS = 1e-5
RNE = 12582912.0
AR = 4
BT = 4
NB = -(-NT // BT)
assert NT == (NB - 1) * BT + 1


class Steps:

    def __init__(self, eng, sem):
        self.eng, self.sem, self.n, self.at = eng, sem, 0, 0

    def done(self, ins):
        ins.then_inc(self.sem, 1)
        self.n += 1

    def wait(self):
        self.eng.wait_ge(self.sem, self.at + self.n)

    def __call__(self, ins):
        self.done(ins)
        self.wait()


def gnn_stack(nc, x, src, dst, ea16, ea6, W0, a0, Wn, bn, Wsf, bs, Wg, Ws, bg, W1, b1, W2, b2, W3, b3, W4, b4, We, be, out):
    ctx = ExitStack()
    with ctx:
        def sb(name, shape, dt=FP32):
            return ctx.enter_context(nc.sbuf_tensor(name, shape, dt))

        def sem(name):
            return ctx.enter_context(nc.semaphore(name))

        def dram(name, shape, dt=FP32):
            return nc.dram_tensor(name, shape, dt, kind="Internal").ap()

        table = dram("table", [NPAD, TW])
        records = dram("records", [CH * NC, W])
        counts = dram("counts", [NT, TS, DW], FP16)

        arenaA = sb("arenaA", [128, NC * W])
        arenaB = sb("arenaB", [128, EC * W])
        arenaC = sb("arenaC", [128, 6 * EC + 500])
        ident = sb("ident", [128, 128])
        identb = sb("identb", [128, 128], BF16)
        ones = sb("ones", [128, 128])
        zerob = sb("zerob", [128, 128], BF16)
        tril = sb("tril", [128, 128])
        degsel = sb("degsel", [128, F])
        iotad = sb("iotad", [128, HW_], FP16)
        iotas = sb("iotas", [128, TS], BF16)
        binid = sb("binid", [128, NBIN])
        xs = sb("xs", [128, NT, F])
        ys = sb("ys", [128, NT, F])
        arenaD = sb("arenaD", [128, 2 * NPAD])
        xT, esum = arenaD[:, 0:NPAD], arenaD[:, NPAD:2 * NPAD]
        w0s = sb("w0s", [F, F])
        w0T = sb("w0T", [F, F])
        ablk = sb("ablk", [F, 2 * HEADS])
        edgeblk = sb("edgeblk", [128, 8 * HEADS])
        wcat = sb("wcat", [F, F + 2 * HEADS])
        wnT = sb("wnT", [F, F])
        wsT = sb("wsT", [F, F])
        wgs = sb("wgs", [F, 2, F])
        w4s = sb("w4s", [F, F])
        wext = sb("wext", [128, F])
        brow1 = sb("brow1", [2, F])
        brow3 = sb("brow3", [1, F])
        bcol = sb("bcol", [F, 1 + 2 * KH])
        ssrc = sb("ssrc", [TS, NT, HEADS])
        s3 = sb("s3", [TS, NT, HEADS, 3], BF16)
        bins = sb("bins", [128, 6, NBIN])
        carry = sb("carry", [EP, NBIN])
        binsi = sb("binsi", [128, NBIN], I32)
        tmap = sb("tmap", [1, NG], I32)
        st = sb("st", [128, 3, NT])
        places = sb("places", [EP, 2, HALF], I32)
        rowid = sb("rowid", [128, 2, SLOTS], I32)
        smalls = sb("smalls", [128, 2, 80])

        ea16s = arenaA[0:EP, 0:EC * EF0]
        rec = arenaB[0:EP, :].rearrange("p (c w) -> p c w", w=W)
        recb = arenaB[0:EP, :].bitcast(BF16).rearrange("p (c w) -> p c w", w=2 * W)
        parts = [arenaC[0:EP, k * EC:(k + 1) * EC] for k in range(6)]
        srci, dsti = parts[0].bitcast(I32), parts[1].bitcast(I32)
        srcf, half, tidf, work, pos = parts[0], parts[1], parts[2], parts[3], parts[4]
        posi = parts[5].bitcast(I32)
        MB = max(BLOCKS)
        binb = parts[0][:, 0:EC // 2].bitcast(BF16)
        masks = [parts[0][:, EC // 2 + k * MB // 2:EC // 2 + (k + 1) * MB // 2] for k in range(2)]
        cums = [parts[1][:, k * MB:(k + 1) * MB] for k in range(2)]
        zero = parts[2][:, 0:MB]
        whole = [parts[2][:, (k + 1) * MB:(k + 2) * MB].bitcast(I32) for k in range(2)]
        eT = arenaC[:, 6 * EC:6 * EC + 4 * EP]
        ein = xT[0:EP, 0:512]
        batch = xT[0:EP, 512:512 + 2 * HALF * W].rearrange("p (h s w) -> p h s w", h=2, s=HALF)
        HE = EC // 2 * EF3
        ysflat = ys[:, :, :].rearrange("p t f -> p (t f)")
        e6h = [ysflat[0:EP, 0:HE], esum[0:EP, 0:HE]]
        TP = 3
        TT = NT // TP
        tpiece = ysflat[0:TS, HE:HE + TT * TW].rearrange("p (t w) -> p t w", w=TW)
        SC = (NPAD - HE) // W
        PADS = -(-NC // SC)
        sent = esum[:, HE:HE + SC * W].rearrange("p (c w) -> p c w", w=W)
        mf = arenaC[0:NT, 0:3 * (NC + 1)].rearrange("p (k c) -> p k c", k=3)
        s3T = arenaC[0:NT, 3 * (NC + 1):3 * (NC + 1) + 6 * TS].bitcast(BF16).rearrange("p (k s) -> p k s", k=12)
        assert 3 * (NC + 1) + 6 * TS <= 5 * EC
        inTile = arenaC[0:NT, 6 * EC:6 * EC + NC // 2].bitcast(BF16)
        endc = bins[0:NT, 0, 0:2]
        beside = bins[0:NT, 1, 0:NT]
        recs = arenaA[:, :].rearrange("p (c w) -> p c w", w=W)
        recsb = arenaA[:, :].bitcast(BF16).rearrange("p (c w) -> p c w", w=2 * W)
        hot = [arenaB[:, s * HW_ // 2:(s + 1) * HW_ // 2].bitcast(FP16) for s in range(2 * GR)]
        o = 2 * GR * HW_ // 2
        stage = arenaB[0:TS, o:o + DW // 2].bitcast(FP16); o += DW // 2
        msg = arenaB[:, o:o + SLOTS * F].rearrange("p (s f) -> p s f", f=F); o += SLOTS * F
        gt = arenaB[:, o:o + SLOTS * TW].rearrange("p (s w) -> p s w", w=TW); o += SLOTS * TW
        assert o <= EC * W
        zerow = arenaC[:, 6 * EC - BANK:6 * EC]
        lut = arenaD[0:TS, 2 * NPAD - NC * 6:2 * NPAD].bitcast(BF16).rearrange("p (c h) -> p c h", h=12)
        o = 0
        stat = arenaC[:, o:o + UN * GR * 64].bitcast(BF16).rearrange("p (s f) -> p s f", f=128); o += UN * GR * 64
        statf = arenaC[:, o:o + SLOTS * TS].rearrange("p (s f) -> p s f", f=TS); o += SLOTS * TS
        dT = arenaC[0:TS, o:o + 2 * GR * 64].bitcast(BF16).rearrange("p (s f) -> p s f", f=128); o += 2 * GR * 64
        assert o <= 6 * EC - BANK
        ring = arenaB[0:TS, 0:AR * DW // 2].bitcast(FP16).rearrange("p (s d) -> p s d", s=AR)
        o = (AR + 1) * DW // 2
        ring0 = arenaB[0:TS, AR * DW // 2:o].bitcast(FP16)
        w1s = arenaB[:, o:o + HID]; o += HID
        w2s = arenaB[:, o:o + KH * HID].rearrange("p (k n) -> p k n", k=KH); o += KH * HID
        w3s = arenaB[:, o:o + KH * F].rearrange("p (k n) -> p k n", k=KH); o += KH * F
        assert o <= EC * W
        scr = arenaC[0:TS, 0:NT * F].rearrange("p (t f) -> p t f", f=F)
        xh = arenaA[0:TS, 0:NT * F // 2].bitcast(FP16).rearrange("p (t f) -> p t f", f=F)
        xl = arenaA[0:TS, NT * F // 2:NT * F].bitcast(FP16).rearrange("p (t f) -> p t f", f=F)
        neT = arenaA[:, NT * F:NT * F + NPAD]
        rdeg = arenaA[:, NT * F + NPAD:NT * F + 2 * NPAD]
        assert NT * F + 2 * NPAD <= NC * W
        BW = BT * TS
        h0 = arenaC[:, 0:BW]
        h1 = arenaC[:, BW:BW * (1 + KH)].rearrange("p (k n) -> p k n", k=KH)
        h2 = arenaC[:, BW * (1 + KH):BW * (1 + 2 * KH)].rearrange("p (k n) -> p k n", k=KH)
        xr, yr = xs[0:TS, :, :], ys[0:TS, :, :]
        ROOTS = [0, NB, 2 * NB, 2 * NB + 1]

        def tiles_of(q):
            return slice(q * BT, min(NT, q * BT + BT))

        def blk(v, q):
            return v[:, tiles_of(q), :]

        acc = [ctx.enter_context(nc.psum_tensor(f"acc{b}", [128, BANK], FP32)) for b in range(8)]
        psT = acc[7][0:TS, 0:256].bitcast(BF16).rearrange("p (j e) -> p j e", j=GR)
        psS = acc[7][:, 256:256 + 2 * GR * HEADS * 3]

        ld_ends, ld_x, ld_e16, ld_e6, ld_w, ld_w2, ld_w3 = (
            sem(n) for n in ("ld_ends", "ld_x", "ld_e16", "ld_e6", "ld_w", "ld_w2", "ld_w3"))
        pool_step, pool_passed, consts, sent_done, e6_split = (sem(n) for n in ("pool_step", "pool_passed", "consts", "sent_done", "e6_split"))
        prep_in, prep_out = sem("prep_in"), sem("prep_out")
        piece_ready, piece_done = sem("piece_ready"), sem("piece_done")
        ein_ready, eT_in, eT_out, el_in, el_out = (sem(n) for n in ("ein_ready", "eT_in", "eT_out", "el_in", "el_out"))
        dve_step = sem("dve_step")
        totals_ready, prefix_in = (sem(n) for n in ("totals_ready", "prefix_in"))
        maps_ready, recs_first, recs_in = sem("maps_ready"), sem("recs_first"), sem("recs_in")
        sp_passed = sem("sp_passed")
        scattered = [sem(f"scattered{h}") for h in range(2)]
        batch_in = [sem(f"batch_in{h}") for h in range(2)]
        gathered = [sem(f"gathered{s}") for s in range(SLOTS)]
        stat_ready, statf_ready, turned, dT_ready = (sem(n) for n in ("stat_ready", "statf_ready", "turned", "dT_ready"))
        src_logits, looked, shifted, exped, msg_ready = (sem(n) for n in ("src_logits", "looked", "shifted", "exped", "msg_ready"))
        hot_ready, main_done, copied, six_out, six_zero, released = (
            sem(n) for n in ("hot_ready", "main_done", "copied", "six_out", "six_zero", "released"))
        half_out, half_stored, half_free = ([sem(f"{n}{h}") for h in ("low", "high")] for n in ("out_", "stored_", "free_"))
        ranked = sem("ranked")
        lut_in, lut_pe, lut_act = (sem(n) for n in ("lut_in", "lut_pe", "lut_act"))
        offs_read, zero_ready, chunk_ids, esum_ready = (sem(n) for n in ("offs_read", "zero_ready", "chunk_ids", "esum_ready"))
        count_in = [sem(f"count_in{s}") for s in range(AR + 1)]
        elu_in, elu_exp, root_in, root_out, x_ready = (sem(n) for n in ("elu_in", "elu_exp", "root_in", "root_out", "x_ready"))
        xh_ready, halves_ready, xT_in, xT_ready = (sem(n) for n in ("xh_ready", "halves_ready", "xT_in", "xT_ready"))
        tile_used, neigh_out, deg_in, deg_out = (sem(n) for n in ("tile_used", "neigh_out", "deg_in", "deg_out"))
        blk_ready, blk_used, out_done = sem("blk_ready"), sem("blk_used"), sem("out_done")
        mlp_in, mlp_out = sem("mlp_in"), sem("mlp_out")

        def groups(left):
            return UN if left is None else min(UN, left)

        def there(k, left):
            return left is None or k < left

        LEFT = [NG - (TURNS - 2) * UN, NG - (TURNS - 1) * UN]


        def load_codes(eng, i, k):
            word = eng.value_load(tmap[0:1, ds(i * UN + k, 1)], min_val=2 << GR, max_val=((NBIN + 2) << (GR + 1)) - 1)
            return word // (2 << GR), word // (1 << GR) % 2, word % (1 << GR)

        def bit(ends, j):
            return ends // (1 << j) % 2

        def code_of(code, ends, j):
            for before in range(j):
                code = code + bit(ends, before)
            return code
        block = ctx.enter_context(nc.Block())

        @block.sync
        def _(sp):
            for lo, hi in ((0, 112), (112, EP)):
                sp.dma_start(srci[lo:hi, :], src.rearrange("(p c) -> p c", p=EP)[lo:hi, :]).then_inc(ld_ends, 16)
                sp.dma_start(dsti[lo:hi, :], dst.rearrange("(p c) -> p c", p=EP)[lo:hi, :]).then_inc(ld_ends, 16)
            sp.wait_ge(consts, 1)
            sp.dma_start(xs[0:TS, 0:NT - 1, :], x[0:TS * (NT - 1), :].rearrange("(t p) f -> p t f", p=TS)).then_inc(ld_x, 16)
            sp.dma_start(xs[0:LAST, NT - 1, :], x[TS * (NT - 1):N, :]).then_inc(ld_x, 16)
            sp.dma_start(w0s[:, :], W0).then_inc(ld_w, 16)
            for h in range(HEADS):
                for k in range(2):
                    sp.dma_start(ablk[HF * h:HF * h + HF, HEADS * (1 - k) + h:HEADS * (1 - k) + h + 1],
                                 a0[h:h + 1, HF * k:HF * k + HF].rearrange("a d -> d a"), allow_slow_non_contiguous=True).then_inc(ld_w, 16)
            for j in range(8):
                sp.dma_start(edgeblk[EF0 * j:EF0 * j + EF0, HEADS * j:HEADS * j + HEADS],
                             a0[:, 2 * HF:2 * HF + EF0].rearrange("h d -> d h"), allow_slow_non_contiguous=True).then_inc(ld_w, 16)
            for lo, hi in ((0, 112), (112, EP)):
                sp.dma_start(ea16s[lo:hi, :], ea16.rearrange("(p c) d -> p (c d)", p=EP)[lo:hi, :]).then_inc(ld_e16, 16)
                for k in range(2):
                    sp.dma_start(e6h[k][lo:hi, :],
                                 ea6.rearrange("(p c) d -> p (c d)", p=EP)[lo:hi, k * HE:(k + 1) * HE]).then_inc(ld_e6, 16)
            for k in range(PADS):
                n = min(SC, NC - k * SC)
                sp.dma_start(records.rearrange("(p c) w -> p c w", c=NC)[:, k * SC:k * SC + n, :],
                             sent[:, 0:n, :]).then_inc(sent_done, 16)
            for to, frm in ((wnT[:, :], Wn), (wsT[:, :], Wsf),
                            (wgs[:, 0, :], Wg), (wgs[:, 1, :], Ws), (w4s[:, :], W4),
                            (brow1[0:1, :], bn.rearrange("(a f) -> a f", a=1)),
                            (brow1[1:2, :], bs.rearrange("(a f) -> a f", a=1)),
                            (brow3[0:1, :], b3.rearrange("(a f) -> a f", a=1)),
                            (bcol[:, 0:1], bg.rearrange("(p a) -> p a", a=1)),
                            (bcol[:, 1:1 + KH], b1.rearrange("(k p) -> p k", p=F)),
                            (bcol[:, 1 + KH:1 + 2 * KH], b2.rearrange("(k p) -> p k", p=F)),
                            (wext[TS:TS + EF3, :], We), (wext[TS + EF3:TS + 2 * EF3, :], We),
                            (wext[TS + 2 * EF3:OCOL, :], We),
                            (wext[OCOL:OCOL + 1, :], b4.rearrange("(a f) -> a f", a=1)),
                            (wext[OCOL + 1:OCOL + 2, :], be.rearrange("(a f) -> a f", a=1))):
                sp.dma_start(to, frm, allow_slow_non_contiguous=True).then_inc(ld_w2, 16)
            sp.wait_ge(e6_split, 1)

            def to_batch(i):
                sp.wait_ge(el_out, i + 1)
                sp.sem_inc(sp_passed, 1)
                for h in range(2):
                    if not (isinstance(i, int) and i == 0):
                        sp.wait_ge(scattered[h], i * (16 * HALF))
                        sp.sem_inc(sp_passed, 1)
                    c0 = i * (2 * HALF) + h * HALF
                    sp.dma_start(places[:, h, :], posi[:, ds(c0, HALF)]).then_inc(batch_in[h], 16)
                    sp.dma_start(batch[:, h, :, :], rec[:, ds(c0, HALF), :]).then_inc(batch_in[h], 16)

            start = 0
            for blk, cols in enumerate(BLOCKS):
                sp.wait_ge(ranked, blk + 1)
                if blk == 0:
                    to_batch(0)
                with sp.Fori(max(1, start // (2 * HALF)), (start + cols) // (2 * HALF)) as i:
                    to_batch(i)
                start += cols
            for h in range(2):
                sp.wait_ge(scattered[h], 8 * EC)
            sp.dma_start(arenaA[:, 0:FIRST * W], records.rearrange("(p c) w -> p (c w)", c=NC)[:, 0:FIRST * W]).then_inc(recs_first, 16)
            sp.dma_start(arenaA[:, FIRST * W:], records.rearrange("(p c) w -> p (c w)", c=NC)[:, FIRST * W:]).then_inc(recs_in, 16)
            for h in range(2):
                sp.sem_inc(half_free[h], 1)
            with sp.Fori(0, NT) as t:
                for h, (lo, hi) in enumerate(((0, LOW), (LOW, DW))):
                    sp.wait_ge(half_out[h], t + 1)
                    sp.dma_start(counts[ds(t, 1), :, lo:hi].rearrange("t p d -> p (t d)"), stage[:, lo:hi]).then_inc(half_stored[h], 16)
                    sp.wait_ge(half_stored[h], t * 16 + 16)
                    sp.sem_inc(half_free[h], 1)
            sp.wait_ge(main_done, NC)
            sp.wait_ge(msg_ready, NG)
            for to, frm in ((w1s, W1), (w2s, W2.rearrange("(k p) n -> p k n", p=F)), (w3s, W3.rearrange("(k p) n -> p k n", p=F))):
                sp.dma_start(to, frm).then_inc(ld_w3, 16)
            for lay in range(3):
                if lay:
                    sp.wait_ge(tile_used, NT * lay)
                sp.dma_start(ring0, counts[0, :, :]).then_inc(count_in[AR], 16)
                for s in range(AR):
                    sp.dma_start(ring[:, s, :], counts[1 + s, :, :]).then_inc(count_in[s], 16)
                with sp.Fori(1, (NT - 1) // AR) as i:
                    for s in range(AR):
                        sp.wait_ge(tile_used, i * AR + (NT * lay + 2 + s - AR))
                        sp.dma_start(ring[:, s, :],
                                     counts[ds(i * AR + (1 + s), 1), :, :].rearrange("t p d -> p (t d)")).then_inc(count_in[s], 16)
            for q in range(NB - 1):
                sp.wait_ge(x_ready, 3 * NB + q + 1)
                sp.dma_start(out[BW * q:BW * (q + 1), :].rearrange("(t p) f -> p t f", p=TS), xs[0:TS, q * BT:(q + 1) * BT, :]).then_inc(out_done, 16)
            sp.wait_ge(x_ready, 4 * NB)
            sp.dma_start(out[TS * (NT - 1):N, :], xs[0:LAST, NT - 1, :]).then_inc(out_done, 16)
            sp.wait_ge(out_done, 16 * NB)

        @block.gpsimd
        def _(pool):
            step = Steps(pool, pool_step)
            step.done(nc.gpsimd.memset(xs[:, NT - 1, :], 0.0))
            step.done(nc.gpsimd.memset(ablk[:, :], 0.0))
            step.done(nc.gpsimd.memset(wext[:, :], 0.0))
            step.done(nc.gpsimd.memset(sent[:, :, :], 0.0))
            step(nc.gpsimd.memset(edgeblk[:, :], 0.0))
            step(nc.gpsimd.memset(sent[:, :, R_DC:R_SL + 1], FAR))
            nc.gpsimd.memset(zerob[:, :], 0.0).then_inc(consts, 1)
            step.done(nc.gpsimd.memset(ones[:, :], 1.0))
            step.done(nc.gpsimd.memset(ident[:, :], 0.0))
            step.done(nc.gpsimd.memset(degsel[:, :], 0.0))
            step(nc.gpsimd.memset(tril[:, :], 1.0))
            step.done(nc.gpsimd.affine_select(out=tril[:, :], in_=tril[:, :], compare_op=ALU.is_gt, fill=0.0,
                                              base=0, pattern=[[1, 128]], channel_multiplier=-1))
            step.done(nc.gpsimd.affine_select(out=degsel[:, :], in_=degsel[:, :], compare_op=ALU.not_equal, fill=1.0,
                                              base=-OCOL, pattern=[[0, F]], channel_multiplier=1))
            step.done(nc.gpsimd.iota(binid[:, :], pattern=[[1, NBIN]], base=0, channel_multiplier=0,
                                     allow_small_or_imprecise_dtypes=True))
            step(nc.gpsimd.affine_select(out=ident[:, :], in_=ident[:, :], compare_op=ALU.not_equal, fill=1.0,
                                         base=0, pattern=[[-1, 128]], channel_multiplier=1))
            nc.gpsimd.tensor_copy(identb[:, :], ident[:, :]).then_inc(consts, 1)
            step.done(nc.gpsimd.iota(iotad[:, :], pattern=[[1, HW_]], base=0, channel_multiplier=0,
                                     allow_small_or_imprecise_dtypes=True))
            step(nc.gpsimd.iota(iotas[:, :], pattern=[[1, TS]], base=0, channel_multiplier=0,
                                     allow_small_or_imprecise_dtypes=True))
            pool.sem_inc(consts, 1)
            pool.wait_ge(ld_e6, 64)
            e = e6h[0].rearrange("p (c d) -> p c d", d=EF3)
            for part in range(3):
                to = recb[:, 0:EC // 2, 2 * R_E6 + EF3 * part:2 * R_E6 + EF3 * (part + 1)]
                step(nc.gpsimd.tensor_copy(to, e))
                if part < 2:
                    step(nc.gpsimd.tensor_tensor(e, e, to, ALU.subtract))
            pool.wait_ge(sent_done, 16 * PADS)
            pool.sem_inc(e6_split, 1)
            def scatter(i):
                for h in range(2):
                    pool.wait_ge(batch_in[h], i * 32 + 32)
                    pool.sem_inc(pool_passed, 1)
                    for s in range(HALF):
                        nc.gpsimd.indirect_dma_start(
                            out=records, out_offset=bass.IndirectOffsetOnAxis(ap=places[:, h, s:s + 1], axis=0),
                            in_=batch[:, h, s, :], in_offset=None).then_inc(scattered[h], 16)

            early = sum(BLOCKS[:3]) // (2 * HALF)
            with pool.Fori(0, early) as i:
                scatter(i)
            pool.wait_ge(ranked, len(BLOCKS))
            nc.gpsimd.iota(mf[:, 1, :], pattern=[[1, NC + 1]], base=0, channel_multiplier=0,
                           allow_small_or_imprecise_dtypes=True).then_inc(chunk_ids, 1)
            with pool.Fori(early, EC // (2 * HALF)) as i:
                scatter(i)
            pool.wait_ge(recs_first, 16)
            pool.wait_ge(piece_done, 16 * TP)

            def row_ids(i, half):
                step(nc.gpsimd.tensor_copy(
                    rowid[:, half, :],
                    recs[:, ds(i * SLOTS, SLOTS), R_DST:R_DST + 1].rearrange("p c w -> p (c w)").bitcast(I32)))
                pool.sem_inc(pool_passed, 1)

            def gather(k, half):
                for s in range(k * GR, (k + 1) * GR):
                    nc.gpsimd.indirect_dma_start(
                        out=gt[:, s, :], out_offset=None, in_=table,
                        in_offset=bass.IndirectOffsetOnAxis(ap=rowid[:, half, s:s + 1], axis=0)).then_inc(gathered[s], 16)

            def gathers(i, half):
                row_ids(i, half)
                for k in range(RG):
                    pool.wait_ge(msg_ready, i * RG + (k + 1 - RG))
                    pool.sem_inc(pool_passed, 1)
                    gather(k, half)

            row_ids(0, 0)
            for k in range(RG):
                gather(k, 0)
            pool.wait_ge(recs_in, 16)
            with pool.Fori(0, (NG // RG - 1) // 2) as i:
                step.at = i * 2
                gathers(i * 2 + 1, 1)
                gathers(i * 2 + 2, 0)
            assert NG // RG % 2 == 1

        @block.tensor
        def _(pe):
            pe.wait_ge(consts, 2)
            pe.wait_ge(totals_ready, 1)
            nc.tensor.matmul(acc[4][0:EP, 0:NBIN], tril[0:EP, 0:EP], bins[0:EP, 0, :], start=True, stop=True)
            nc.tensor.matmul(acc[4][:, 128:128 + NBIN], ones[0:EP, :], bins[0:EP, 0, :], start=True, stop=True).then_inc(prefix_in, 1)
            pe.wait_ge(ld_w, 16 * (1 + 2 * HEADS + 8))
            nc.tensor.transpose(acc[0][:, 0:F], w0s[:, :], ident[:, :]).then_inc(prep_in, 1)
            pe.wait_ge(prep_out, 1)
            nc.tensor.matmul(acc[1][:, 0:2 * HEADS], w0T[:, :], ablk[:, :], start=True, stop=True).then_inc(prep_in, 1)
            pe.wait_ge(ld_w2, 16 * 16)
            nc.tensor.transpose(acc[2][:, 0:F], wnT[:, :], ident[:, :]).then_inc(prep_in, 1)
            nc.tensor.transpose(acc[3][:, 0:F], wsT[:, :], ident[:, :]).then_inc(prep_in, 1)
            pe.wait_ge(prep_out, 4)
            pe.wait_ge(ld_x, 32)
            pe.wait_ge(offs_read, 1)

            def turn_x(q, first):
                if q == 8:
                    pe.wait_ge(xT_ready, first + 1)
                for t in range(q * BT, min(NT, q * BT + BT)):
                    last = nc.tensor.transpose(acc[(q + 7) % 8][:, (t % BT) * TS:(t % BT + 1) * TS], xs[0:TS, t, :], ident[0:TS, 0:TS])
                last.then_inc(xT_in, 1)

            for q in range(NB):
                turn_x(q, 0)
            pe.wait_ge(xT_ready, NB)
            for t in range(NT):
                if t >= 4:
                    pe.wait_ge(prep_out, 4 + t - 3)
                nc.tensor.matmul(acc[t % 4][0:TS, 0:F + 2 * HEADS], xT[:, t * TS:(t + 1) * TS], wcat[:, :],
                                 start=True, stop=True).then_inc(prep_in, 1)

            def edge_logits(i):
                pe.wait_ge(ein_ready, i + 1)
                for k in range(4):
                    last = nc.tensor.transpose(acc[5][:, k * EP:(k + 1) * EP], ein[:, k * 128:(k + 1) * 128], ident[0:EP, 0:EP])
                last.then_inc(eT_in, 1)
                pe.wait_ge(eT_out, i + 1)
                for k in range(4):
                    last = nc.tensor.matmul(acc[6][0:EP, k * 32:(k + 1) * 32], eT[:, k * EP:(k + 1) * EP], edgeblk[:, :],
                                            start=True, stop=True)
                last.then_inc(el_in, 1)

            with pe.Fori(0, EC // 32) as i:
                edge_logits(i)

            pe.wait_ge(lut_in, 1)
            for k in range(12):
                last = nc.tensor.transpose(acc[k // 6][0:NT, :].bitcast(BF16)[:, (k % 6) * TS:(k % 6 + 1) * TS],
                                           s3[:, :, :, :].rearrange("p t h k -> p t (h k)")[:, :, k], identb[0:TS, 0:TS])
            last.then_inc(lut_pe, 1)
            pe.wait_ge(lut_act, 1)
            for k in range(24):
                if k >= 4:
                    pe.wait_ge(lut_act, k - 2)
                nc.tensor.matmul(acc[k % 4][0:TS, 0:NC // 2], s3T[:, k // 2, :], inTile[:, (k % 2) * (NC // 2):(k % 2 + 1) * (NC // 2)],
                                 start=True, stop=True).then_inc(lut_pe, 1)
            pe.wait_ge(lut_act, 25)
            pe.wait_ge(el_out, EC // 32)
            pe.wait_ge(prep_out, 4 + NT)
            pe.wait_ge(offs_read, 1)
            pe.wait_ge(zero_ready, 1)
            for b in range(7):
                last = nc.tensor.matmul(acc[b][:, :], zerob[:, :], zerow[:, :].bitcast(BF16)[:, 0:BANK], start=True, stop=False, skip_group_check=True)

            def turn_stat(i, k):
                pe.wait_ge(stat_ready, i * UN + k + 1)
                if k % 2 == 0 and not (isinstance(i, int) and i * UN + k == 0):
                    pe.wait_ge(looked, i * (UN // 2) + k // 2)
                for j in range(GR):
                    last = nc.tensor.transpose(psT[:, j, :], stat[:, (k % UN) * GR + j, 0:TS], identb[:, :])
                last.then_inc(turned, 1)

            def look_up(i, k):
                pe.wait_ge(dT_ready, i * UN + k + 1)
                for j in range(GR):
                    c = (i * UN + k) * GR + j
                    at = (k % 2) * GR + j
                    last = nc.tensor.matmul(psS[:, at * 12:(at + 1) * 12], dT[:, at, :],
                                            lut[:, ds(c, 1), :].rearrange("p c h -> p (c h)"), start=True, stop=True)
                last.then_inc(src_logits, 1)

            def products(i, k, j, high):
                s = (k % UN) * GR + j
                pe.wait_ge(hot_ready, (i * UN + k) * GR + (j + 1))
                for b, (at, n) in enumerate(DB[HB:] if high else DB[:HB]):
                    nc.tensor.matmul(acc[b + HB * high][:, 0:n], stat[:, s, :], hot[k % 2 * GR + j][:, b * BANK:b * BANK + n],
                                     start=False, stop=False, skip_group_check=True)
                ring_slot = (k % RG) * GR + j
                nc.tensor.matmul(acc[6][0:TS, HCOL:HCOL + F], statf[:, ring_slot, :], msg[:, ring_slot, :],
                                 start=False, stop=False, skip_group_check=True).then_inc(main_done, 1)

            def group(i, k, left, chunk):
                for j in range(GR):
                    chunk(j)
                    if k % 2 == 0 and j == 0 and there(k + 4, left):
                        look_up(i, k + 4)
                    if j == (3 if k % 2 else 0) and there(k + 5, left):
                        turn_stat(i, k + 5)
                    if k % 2 == 0 and j == 2 and there(k + 5, left):
                        look_up(i, k + 5)

            def turn(i, left=None):
                for k in range(groups(left)):
                    pe.wait_ge(msg_ready, i * UN + k + 1)
                    pe.wait_ge(statf_ready, i * UN + k + 1)
                    code, _, ends = load_codes(pe, i, k)
                    with pe.If(ends % (1 << (GR - 1)) != 0):
                        def chunk(j):
                            own = code_of(code, ends, j)
                            pe.wait_ge(released, own)
                            with pe.If(own % 2 == 1):
                                products(i, k, j, 0)
                            with pe.Else():
                                products(i, k, j, 1)
                        group(i, k, left, chunk)
                    with pe.Else():
                        pe.wait_ge(released, code)
                        with pe.If(code % 2 == 1):
                            group(i, k, left, lambda j: products(i, k, j, 0))
                        with pe.Else():
                            group(i, k, left, lambda j: products(i, k, j, 1))

            for k in range(4):
                turn_stat(0, k)
                look_up(0, k)
            turn_stat(0, 4)
            turn(0)
            with pe.Fori(1, TURNS - 2) as i:
                turn(i)
            for n, left in enumerate(LEFT):
                turn(TURNS - 2 + n, left)

            pe.wait_ge(esum_ready, 2)
            for b, (at, n) in enumerate(DB):
                last = nc.tensor.matmul(acc[b][:, 0:n], degsel[TS:128, :], esum[TS:128, at:at + n], start=True, stop=True)
            last.then_inc(deg_in, 1)
            pe.wait_ge(deg_out, 1)
            for lay in range(3):
                if lay:
                    pe.wait_ge(blk_used, NB * lay)

                def first_layer(q):
                    n = min(NT - q * BT, BT) * TS
                    cols = slice(q * BW, q * BW + n)
                    nc.tensor.matmul(acc[1][:, 0:n], wgs[:, 0, :], neT[:, cols], start=True, stop=False)
                    nc.tensor.matmul(acc[1][:, 0:n], wgs[:, 1, :], xT[:, cols], start=False, stop=True).then_inc(mlp_in, 1)

                def count_tile(k, tile, start):
                    for h, half in enumerate((xh, xl)):
                        for b, (at, n) in enumerate(DB):
                            last = nc.tensor.matmul(acc[b][:, 0:n], half[:, ds(k, 1), :].rearrange("p t f -> p (t f)"),
                                                    tile[:, at:at + n], start=start and h == 0, stop=False,
                                                    skip_group_check=True)
                    last.then_inc(tile_used, 1)

                pe.wait_ge(halves_ready, NB * lay + 1)
                pe.wait_ge(count_in[AR], 16 * (lay + 1))
                count_tile(0, ring0, True)
                with pe.Fori(0, (NT - 1) // AR) as i:
                    for s in range(AR):
                        if (1 + s) % BT == 0:
                            pe.wait_ge(halves_ready, i + (NB * lay + 2))
                        pe.wait_ge(count_in[s], i * 16 + 16 * (lay * ((NT - 1) // AR) + 1))
                        count_tile(i * AR + (1 + s), ring[:, s, :], False)
                if lay < 2:
                    for q in range(NB):
                        if q == 1:
                            pe.wait_ge(neigh_out, 7 * (lay + 1))
                        turn_x(q, NB * (lay + 1))
                    pe.wait_ge(xT_ready, NB * (lay + 2))
                pe.wait_ge(neigh_out, 7 * (lay + 1))
                if lay == 1:
                    first_layer(0)
                for q in range(NB):
                    tiles = range(q * BT, min(NT, q * BT + BT))
                    n = len(tiles) * TS
                    if lay == 1:
                        at = 9 * q
                        pe.wait_ge(mlp_out, at + 1)
                        if q == 0:
                            pe.wait_ge(ld_w3, 48)
                        for m in MLP_ORDER:
                            if q and m == 0:
                                pe.wait_ge(blk_used, NB + q)
                            nc.tensor.matmul(acc[m][:, 0:n], w1s[:, m * F:(m + 1) * F], h0[:, 0:n], start=True, stop=True).then_inc(mlp_in, 1)
                        for m in range(KH):
                            for u, k in enumerate(MLP_ORDER):
                                if m == 0:
                                    pe.wait_ge(mlp_out, at + 2 + u)
                                last = nc.tensor.matmul(acc[4 + m][:, 0:n], w2s[:, k, m * F:(m + 1) * F], h1[:, k, 0:n],
                                                        start=u == 0, stop=u == KH - 1)
                            last.then_inc(mlp_in, 1)
                        if q + 1 < NB:
                            first_layer(q + 1)
                        pe.wait_ge(mlp_out, at + 9)
                        bank = 0
                    else:
                        bank = q % 8
                        if q == 8:
                            pe.wait_ge(blk_used, NB * lay + 1)
                    for j, t in enumerate(tiles):
                        to = acc[bank][0:TS, j * F:(j + 1) * F]
                        tc_ = slice(t * TS, (t + 1) * TS)
                        if lay == 0:
                            nc.tensor.matmul(to, neT[:, tc_], wnT[:, :], start=True, stop=False)
                            nc.tensor.matmul(to, xT[:, tc_], wsT[:, :], start=False, stop=False)
                            last = nc.tensor.matmul(to, ones[0:2, 0:TS], brow1[:, :], start=False, stop=True)
                        elif lay == 1:
                            for k in range(KH):
                                nc.tensor.matmul(to, h2[:, k, j * TS:(j + 1) * TS], w3s[:, k, :], start=k == 0, stop=False)
                            last = nc.tensor.matmul(to, ones[0:1, 0:TS], brow3[:, :], start=False, stop=True)
                        else:
                            nc.tensor.matmul(to, neT[:, tc_], w4s[:, :], start=True, stop=False)
                            last = nc.tensor.matmul(to, esum[TS:128, tc_], wext[TS:128, :], start=False, stop=True)
                    last.then_inc(blk_ready, 1)

        @block.scalar
        def _(act):
            act.wait_ge(prep_in, 1)
            nc.scalar.copy(w0T[:, :], acc[0][:, 0:F]).then_inc(prep_out, 1)
            act.wait_ge(prep_in, 2)
            nc.scalar.copy(wcat[:, 0:F], w0s[:, :])
            nc.scalar.copy(wcat[:, F:F + 2 * HEADS], acc[1][:, 0:2 * HEADS]).then_inc(prep_out, 1)
            act.wait_ge(prep_in, 4)
            nc.scalar.copy(wnT[:, :], acc[2][:, 0:F]).then_inc(prep_out, 1)
            nc.scalar.copy(wsT[:, :], acc[3][:, 0:F]).then_inc(prep_out, 1)

            def copy_xT(first):
                for q in range(NB):
                    n = min(NPAD - q * BW, BW)
                    act.wait_ge(xT_in, first + q + 1)
                    nc.scalar.copy(xT[:, q * BW:q * BW + n], acc[(q + 7) % 8][:, 0:n]).then_inc(xT_ready, 1)

            copy_xT(0)
            for t in range(NT):
                if t and t % TT == 0:
                    act.wait_ge(piece_done, 16 * (t // TT))
                act.wait_ge(prep_in, 4 + t + 1)
                ins = nc.scalar.copy(tpiece[:, t % TT, :], acc[t % 4][0:TS, 0:TW])
                if t % TT == TT - 1:
                    ins.then_inc(piece_ready, 1)
                nc.scalar.copy(ssrc[:, t, :], acc[t % 4][0:TS, TW:TW + HEADS]).then_inc(prep_out, 1)
                if t % TT == TT - 1:
                    k = t // TT
                    act.wait_ge(piece_ready, k + 1)
                    nc.scalar.dma_start(table[k * TT * TS:(k + 1) * TT * TS, :].rearrange("(t p) f -> p t f", p=TS),
                                        tpiece).then_inc(piece_done, 16)

            act.wait_ge(ld_e16, 32)

            def edge_logits(i):
                nc.scalar.copy(ein[:, :], ea16s[:, ds(i * 512, 512)]).then_inc(ein_ready, 1)
                act.wait_ge(eT_in, i + 1)
                nc.scalar.copy(eT[:, :], acc[5][:, 0:4 * EP]).then_inc(eT_out, 1)
                act.wait_ge(el_in, i + 1)
                nc.scalar.copy(rec[:, ds(i * 32, 32), R_EA:R_EA + HEADS],
                               acc[6][0:EP, 0:128].rearrange("p (c h) -> p c h", h=HEADS)).then_inc(el_out, 1)

            with act.Fori(0, EC // 32) as i:
                edge_logits(i)

            def exp_pair(i, k):
                at = (k // 2) % 2
                act.wait_ge(shifted, i * (UN // 2) + k // 2 + 1)
                nc.scalar.activation(smalls[:, at, 32:64], smalls[:, at, 0:32], ACT.Exp).then_inc(exped, 1)

            def copy_turned(i, k):
                act.wait_ge(turned, i * UN + k + 1)
                s = (k % 2) * GR
                nc.scalar.copy(dT[:, s:s + GR, :], psT[:, :, :]).then_inc(dT_ready, 1)

            def copy_stat(i, k):
                act.wait_ge(stat_ready, i * UN + k + 1)
                if not (isinstance(i, int) and i * UN + k < RG):
                    act.wait_ge(main_done, (i * UN + k) * GR - (RG - 1) * GR)
                to, frm = (k % RG) * GR, (k % UN) * GR
                nc.scalar.copy(statf[:, to:to + GR, :], stat[:, frm:frm + GR, 0:TS]).then_inc(statf_ready, 1)

            def evacuate(code, high):
                banks = list(enumerate(DB))[HB:2 * HB] if high else list(enumerate(DB))[:HB]
                for b, (at, n) in banks:
                    last = nc.scalar.mul(stage[:, at:at + n], acc[b][0:TS, 0:n], CS)
                last.then_inc(copied, 1)
                act.wait_ge(copied, code)
                for b, (at, n) in banks:
                    last = nc.scalar.copy(acc[b][0:TS, 0:n], zerow[0:TS, 0:n])
                last.then_inc(half_out[high], 1)

            def order_of(code):
                return nc.s_assert_within((code + 1) // 2, 1, NT,
                                          skip_runtime_bounds_check_because="only real bins have ends, and there are 2 NT")

            def lower_end(code):
                act.wait_ge(half_free[0], order_of(code))
                evacuate(code, 0)

            def bank_six(code):
                order = order_of(code)
                act.wait_ge(half_free[1], order)
                nc.scalar.mul(stage[:, 2 * LOW:DW], acc[6][0:TS, 0:DW - 2 * LOW], CS)
                nc.scalar.copy(ys[0:TS, ds(order - 1, 1), :].rearrange("p t f -> p (t f)"), acc[6][0:TS, HCOL:HCOL + F]).then_inc(six_out, 1)
                act.wait_ge(six_out, order)
                nc.scalar.copy(acc[6][0:TS, 0:HCOL + F], zerow[0:TS, 0:HCOL + F]).then_inc(six_zero, 1)
                act.wait_ge(six_zero, order)
                act.wait_ge(half_out[0], order)
                act.sem_inc(released, 1)

            def upper_end(code):
                evacuate(code, 1)
                act.wait_ge(half_out[1], order_of(code))
                act.sem_inc(released, 1)

            def finish(i, k, code, single):
                with act.If(single == 1):
                    act.wait_ge(main_done, (i * UN + k) * GR)
                    with act.If(code % 2 == 1):
                        lower_end(code)
                    with act.Else():
                        upper_end(code)

            def ends_of(i, k, code, single, ends):
                with act.If(ends != 0):
                    with act.If(single == 1):
                        with act.If(code % 2 == 0):
                            act.wait_ge(main_done, (i * UN + k) * GR + 1 + ends // 2 % 4 + ends // 8 * 3)
                            bank_six(code)
                    with act.Else():
                        for j in range(GR):
                            with act.If(bit(ends, j) == 1):
                                own = code_of(code, ends, j)
                                act.wait_ge(main_done, (i * UN + k) * GR + (j + 1))
                                with act.If(own % 2 == 1):
                                    lower_end(own)
                                with act.Else():
                                    bank_six(own)
                                    upper_end(own)

            def turn(i, left=None):
                before = None
                if not (isinstance(i, int) and i == 0):
                    before = load_codes(act, i, -1)
                for k in range(groups(left)):
                    now = load_codes(act, i, k)
                    if k % 2 == 0 and there(k + 2, left):
                        exp_pair(i, k + 2)
                    if k % 2 == 0 and there(k + 4, left):
                        copy_turned(i, k + 4)
                    if there(k + 2, left):
                        copy_stat(i, k + 2)
                    if k % 2 == 0 and there(k + 5, left):
                        copy_turned(i, k + 5)
                    if before:
                        finish(i, k, *before[:2])
                    ends_of(i, k, *now)
                    before = now
                if left is not None and left <= UN:
                    finish(i, groups(left), *before[:2])

            act.wait_ge(lut_pe, 1)
            for k in range(2):
                last = nc.scalar.copy(s3T[:, k * 6:k * 6 + 6, :], acc[k][0:NT, :].bitcast(BF16)[:, 0:6 * TS].rearrange("p (k s) -> p k s", k=6))
            last.then_inc(lut_act, 1)
            for k in range(24):
                act.wait_ge(lut_pe, k + 2)
                last = nc.scalar.copy(lut[:, (k % 2) * (NC // 2):(k % 2 + 1) * (NC // 2), k // 2], acc[k % 4][0:TS, 0:NC // 2])
                last.then_inc(lut_act, 1)
            act.wait_ge(lut_act, 25)
            act.sem_inc(lut_in, 1)
            act.wait_ge(maps_ready, 1)
            act.sem_inc(released, 2)
            for k in range(4):
                copy_turned(0, k)
                if k == 1:
                    exp_pair(0, 0)
            for k in range(2):
                copy_stat(0, k)
            turn(0)
            with act.Fori(1, TURNS - 2) as i:
                turn(i)
            for n, left in enumerate(LEFT):
                turn(TURNS - 2 + n, left)
            act.wait_ge(main_done, NC)
            for b, (at, n) in enumerate(DB):
                last = nc.scalar.copy(esum[TS:128, at:at + n], acc[b][TS:128, 0:n])
            last.then_inc(esum_ready, 1)

            for q in range(NB):
                act.wait_ge(elu_in, q + 1)
                nc.scalar.activation(blk(scr, q), blk(scr, q), ACT.Exp).then_inc(elu_exp, 1)
            act.wait_ge(deg_in, 1)
            for b, (at, n) in enumerate(DB):
                last = nc.scalar.copy(rdeg[:, at:at + n], acc[b][:, 0:n])
            last.then_inc(deg_out, 1)

            def root(lay, q):
                act.wait_ge(root_in, ROOTS[lay] + (q or 0) + 1)
                own = slice(0, NT) if q is None else tiles_of(q)
                nc.scalar.activation(st[0:TS, 1, own], st[0:TS, 0, own], ACT.Sqrt).then_inc(root_out, 1)

            def high_half(lay, q):
                act.wait_ge(x_ready, NB * lay + q + 1)
                nc.scalar.mul(blk(xh, q), blk(xr, q), XS).then_inc(xh_ready, 1)

            for lay in range(4):
                if lay == 2:
                    root(lay, None)
                for q in range(NB + 1):
                    if lay != 2 and q < NB:
                        root(lay, q)
                    if lay < 3 and q:
                        high_half(lay, q - 1)
                if lay == 3:
                    break
                if lay != 1:
                    act.wait_ge(tile_used, NT * (lay + 1))
                    for b, (at, n) in enumerate(DB):
                        nc.scalar.mul(neT[:, at:at + n], acc[b][:, 0:n], 1.0 / (CS * XS)).then_inc(neigh_out, 1)
                if lay < 2:
                    copy_xT(NB * (lay + 1))
                if lay == 1:
                    for q in range(NB):
                        n = min(NPAD - q * BW, BW)
                        at = 9 * q
                        act.wait_ge(mlp_in, at + 1)
                        nc.scalar.activation(h0[:, 0:n], acc[1][:, 0:n], ACT.Relu, bias=bcol[:, 0:1]).then_inc(mlp_out, 1)
                        for u, m in enumerate(MLP_ORDER):
                            act.wait_ge(mlp_in, at + 2 + u)
                            nc.scalar.activation(h1[:, m, 0:n], acc[m][:, 0:n], ACT.Tanh, bias=bcol[:, 1 + m:2 + m]).then_inc(mlp_out, 1)
                        for m in range(KH):
                            act.wait_ge(mlp_in, at + 6 + m)
                            nc.scalar.activation(h2[:, m, 0:n], acc[4 + m][:, 0:n], ACT.Tanh, bias=bcol[:, 1 + KH + m:2 + KH + m]).then_inc(mlp_out, 1)

        @block.vector
        def _(dve):
            step = Steps(dve, dve_step)
            V = nc.vector
            dve.wait_ge(ld_ends, 64)
            step.done(V.tensor_copy(rec[:, :, R_DST].bitcast(I32), dsti))
            step.done(V.tensor_copy(work, srci))
            step.done(V.tensor_scalar(pos, dsti, float(LOW), -float(LOW), ALU.is_ge, ALU.mult))
            step(V.tensor_scalar(posi, srci, 5, None, ALU.logical_shift_right))
            step.done(V.tensor_tensor(rec[:, :, R_DC], pos, dsti, ALU.add))
            step(V.tensor_scalar(tidf, posi, 1.0 / 3, -1.0 / 3, ALU.mult, ALU.add))
            step(V.tensor_scalar(tidf, tidf, RNE, None, ALU.add))
            step(V.tensor_scalar(tidf, tidf, -RNE, None, ALU.add))
            step(V.scalar_tensor_tensor(rec[:, :, R_SL], tidf, float(-TS), work, ALU.mult, ALU.add))
            step.done(V.tensor_scalar(half, pos, -1023.0 / LOW, 1.0, ALU.mult, ALU.add))
            step(V.tensor_scalar(work, pos, -0.5 / LOW, None, ALU.mult))
            step.done(V.tensor_tensor(work, work, tidf, ALU.add))
            dve.wait_ge(consts, 2)
            step.wait()
            for t in range(NT):
                step(V.scalar_tensor_tensor(pos, tidf, binid[0:EP, t:t + 1], half, ALU.is_equal, ALU.mult,
                                            accum_out=bins[0:EP, 1, t:t + 1]))
            step(V.tensor_copy(binsi[0:EP, 0:NT], bins[0:EP, 1, 0:NT]))
            step.done(V.tensor_scalar(binsi[0:EP, NT:NBIN], binsi[0:EP, 0:NT], 10, None, ALU.logical_shift_right))
            step.done(V.tensor_scalar(binb, work, 2.0, None, ALU.mult))
            step(V.tensor_scalar(binsi[0:EP, 0:NT], binsi[0:EP, 0:NT], 1023, None, ALU.bitwise_and))
            step.done(V.memset(zero, 0.0))
            V.tensor_copy(bins[0:EP, 0, :].rearrange("p (t h) -> p h t", h=2),
                          binsi[0:EP, :].rearrange("p (h t) -> p h t", h=2)).then_inc(totals_ready, 1)
            dve.wait_ge(totals_ready, 1)
            step.wait()
            dve.wait_ge(prefix_in, 1)
            step(V.tensor_scalar(bins[:, 2, :], acc[4][:, 128:128 + NBIN], float(CH - 1), None, ALU.add))
            step(V.tensor_copy(binsi[:, :], bins[:, 2, :]))
            step(V.tensor_scalar(binsi[:, :], binsi[:, :], 7, None, ALU.logical_shift_right))
            step.done(V.memset(bins[:, 5, :], 0.0))
            step(V.tensor_copy(bins[:, 3, :], binsi[:, :]))
            step(V.tensor_scalar(bins[:, 3, :], bins[:, 3, :], 1.0, None, ALU.max))
            step(V.tensor_tensor_scan(bins[:, 4, :], bins[:, 3, :], bins[:, 5, :], 0.0, ALU.add, ALU.add))
            step(V.tensor_tensor(bins[:, 2, :], bins[:, 4, :], bins[:, 3, :], ALU.subtract))
            step(V.tensor_scalar(bins[:, 2, :], bins[:, 2, :], float(CH), -1.0, ALU.mult, ALU.add))
            V.tensor_tensor(carry[:, :], bins[0:EP, 2, :], acc[4][0:EP, 0:NBIN], ALU.add).then_inc(offs_read, 1)
            dve.wait_ge(offs_read, 1)
            start = 0
            for cols in BLOCKS:
                at = slice(start, start + cols)
                for b in range(0, NBIN, 2):
                    for u in range(2):
                        step.done(V.tensor_scalar(masks[u].bitcast(BF16)[:, 0:cols], binb[:, at], binid[0:EP, b + u:b + u + 1], None, ALU.is_equal))
                    step.wait()
                    for u in range(2):
                        step.done(V.tensor_tensor_scan(cums[u][:, 0:cols], masks[u].bitcast(BF16)[:, 0:cols], zero[:, 0:cols],
                                                       carry[:, b + u:b + u + 1], ALU.add, ALU.add))
                    step.wait()
                    for u in range(2):
                        step.done(V.tensor_copy(carry[:, b + u:b + u + 1], cums[u][:, cols - 1:cols]))
                        step(V.copy_predicated(pos[:, at], masks[u].bitcast(mybir.dt.int16)[:, 0:cols], cums[u][:, 0:cols]))
                step(V.tensor_copy(posi[:, at], pos[:, at]))
                step.done(V.tensor_scalar(whole[0][:, 0:cols], posi[:, at], CH - 1, None, ALU.bitwise_and))
                step(V.tensor_scalar(whole[1][:, 0:cols], posi[:, at], 7, None, ALU.logical_shift_right))
                step.done(V.tensor_copy(cums[0][:, 0:cols], whole[0][:, 0:cols]))
                step(V.tensor_copy(cums[1][:, 0:cols], whole[1][:, 0:cols]))
                step(V.scalar_tensor_tensor(pos[:, at], cums[0][:, 0:cols], float(NC), cums[1][:, 0:cols], ALU.mult, ALU.add))
                V.tensor_copy(posi[:, at], pos[:, at]).then_inc(ranked, 1)
                start += cols
                if start == sum(BLOCKS[:3]):
                    dve.wait_ge(ld_e6, 64)
                    e = e6h[1].rearrange("p (c d) -> p c d", d=EF3)
                    for part in range(3):
                        to = recb[:, EC // 2:EC, 2 * R_E6 + EF3 * part:2 * R_E6 + EF3 * (part + 1)]
                        step(V.tensor_copy(to, e))
                        if part < 2:
                            step(V.tensor_tensor(e, e, to, ALU.subtract))
            dve.wait_ge(ranked, len(BLOCKS))
            dve.wait_ge(prep_out, 4 + NT)
            for part in range(3):
                step(V.tensor_copy(s3[:, :, :, part], ssrc[:, :, :]))
                if part < 2:
                    step(V.tensor_tensor(ssrc[:, :, :], ssrc[:, :, :], s3[:, :, :, part], ALU.subtract))
            step(V.memset(mf[0:1, 0, :], 0.0))
            dve.wait_ge(chunk_ids, 1)
            for k in range(2):
                if k:
                    step(V.tensor_copy(beside, bins[0:NT, 4, 1:NBIN:2]))
                    step(V.memset(beside[:, NT - 1:NT], FAR))
                else:
                    step(V.tensor_tensor(beside, bins[0:NT, 4, 0:NBIN:2], bins[0:NT, 3, 0:NBIN:2], ALU.subtract))
                step(V.tensor_tensor(bins[0:NT, 2, 0:NT], beside, ident[0:NT, 0:NT], ALU.mult))
                step(V.tensor_reduce(endc[:, k:k + 1], bins[0:NT, 2, 0:NT], AX, ALU.add))
            step(V.tensor_scalar(mf[:, 2, 0:NC], mf[:, 1, 0:NC], endc[:, 0:1], None, ALU.is_ge))
            dve.wait_ge(el_out, EC // 32)
            V.scalar_tensor_tensor(inTile, mf[:, 1, 0:NC], endc[:, 1:2], mf[:, 2, 0:NC], ALU.is_lt, ALU.mult).then_inc(lut_in, 1)
            for b in range(NBIN):
                step(V.scalar_tensor_tensor(mf[0:1, 0, :], mf[0:1, 1, :], bins[0:1, 4, b:b + 1], mf[0:1, 0, :], ALU.is_ge, ALU.add))
            m4 = mf[0:1, 0, 0:NC].rearrange("p (g j) -> p g j", j=GR)
            e4 = mf[0:1, 0, 1:NC + 1].rearrange("p (g j) -> p g j", j=GR)
            n4 = mf[0:1, 2, 0:NC].rearrange("p (g j) -> p g j", j=GR)
            step.done(V.tensor_tensor(n4, e4, m4, ALU.subtract))
            step(V.tensor_tensor(mf[0:1, 1, 0:NG].rearrange("p (g j) -> p g j", j=1), e4[:, :, GR - 1:GR], m4[:, :, 0:1], ALU.subtract))
            step(V.tensor_scalar(mf[0:1, 1, 0:NG], mf[0:1, 1, 0:NG], 1.0, float(1 << GR), ALU.is_equal, ALU.mult))
            for j in range(1, GR):
                step(V.scalar_tensor_tensor(n4[:, :, 0:1], n4[:, :, j:j + 1], float(1 << j), n4[:, :, 0:1], ALU.mult, ALU.add))
            step(V.scalar_tensor_tensor(n4[:, :, 0:1], m4[:, :, 0:1], float(2 << GR), n4[:, :, 0:1], ALU.mult, ALU.add))
            step(V.scalar_tensor_tensor(tmap[:, :].rearrange("p (g j) -> p g j", j=1), n4[:, :, 0:1], float(2 << GR),
                                        mf[0:1, 1, 0:NG].rearrange("p (g j) -> p g j", j=1), ALU.add, ALU.add))
            dve.wait_ge(lut_in, 2)
            step(V.memset(stat[:, :, :], 0.0))
            V.memset(stat[:, :, OCOL:OCOL + 2], 1.0).then_inc(maps_ready, 1)
            dve.wait_ge(maps_ready, 1)
            dve.wait_ge(consts, 3)
            dve.wait_ge(recs_first, 16)
            V.memset(zerow[:, :], 0.0).then_inc(zero_ready, 1)

            def stat_tiles(i, k):
                s = (k % UN) * GR
                if not (isinstance(i, int) and i * UN + k < UN):
                    dve.wait_ge(main_done, (i * UN + k) * GR - (UN - 1) * GR)
                V.tensor_tensor(stat[:, s:s + GR, 0:TS],
                                iotas[:, :].rearrange("p (a f) -> p a f", a=1).to_broadcast([128, GR, TS]),
                                recs[:, ds((i * UN + k) * GR, GR), R_SL:R_SL + 1].to_broadcast([128, GR, TS]), ALU.is_equal)

            def stat_features(i, k):
                s = (k % UN) * GR
                V.tensor_copy(stat[:, s:s + GR, TS:OCOL],
                              recsb[:, ds((i * UN + k) * GR, GR), 2 * R_E6:2 * R_E6 + E6C]).then_inc(stat_ready, 1)

            def one_hot(i, k, j):
                c = (i * UN + k) * GR + j
                if not (isinstance(i, int) and c < 2 * GR):
                    dve.wait_ge(main_done, c - (2 * GR - 1))
                V.tensor_scalar(hot[k % 2 * GR + j], iotad[:, :], recs[:, ds(c, 1), R_DC:R_DC + 1].rearrange("p c w -> p (c w)"),
                                None, ALU.is_equal).then_inc(hot_ready, 1)

            PER_TURN = 7 * (UN // 2)

            def attention(i, k, hots=False, left=0):
                s, at = (k % RG) * GR, (k // 2) % 2
                z, e = smalls[:, at, 0:32], smalls[:, at, 32:64]
                m, n = smalls[:, at, 64:72], smalls[:, at, 72:80]
                z3, e3 = z.rearrange("p (j h) -> p j h", h=HEADS), e.rearrange("p (j h) -> p j h", h=HEADS)
                over = [v.rearrange("p (j a) -> p j a", a=1).to_broadcast([128, 2 * GR, HEADS]) for v in (m, n)]
                if hots:
                    one_hot(i, k - 2, 0)
                dve.wait_ge(src_logits, i * UN + k + 2)
                V.tensor_reduce(z, psS[:, :].rearrange("p (a b) -> p a b", b=3), AX, ALU.add).then_inc(looked, 1)
                if hots:
                    one_hot(i, k - 2, 1)
                dve.wait_ge(looked, i * (UN // 2) + k // 2 + 1)
                step.done(V.tensor_tensor(z3, z3, recs[:, ds((i * UN + k) * GR, 2 * GR), R_EA:R_EA + HEADS], ALU.add))
                step.wait()
                for j in range(2 * GR):
                    dve.wait_ge(gathered[s + j], i * (16 * UN // RG) + 16 * (k // RG + 1))
                step.done(V.tensor_tensor(z3, z3, gt[:, s:s + 2 * GR, F:TW], ALU.add))
                if there(k + 3, left):
                    stat_tiles(i, k + 3)
                step.wait()
                step.done(V.scalar_tensor_tensor(z, z, ALPHA, z, ALU.mult, ALU.max))
                if there(k + 3, left):
                    stat_features(i, k + 3)
                step.wait()
                step.done(V.tensor_reduce(m, z3, AX, ALU.max))
                if hots:
                    one_hot(i, k - 2, 2)
                step.wait()
                V.tensor_tensor(z3, z3, over[0], ALU.subtract).then_inc(shifted, 1)
                if hots:
                    one_hot(i, k - 2, 3)
                if there(k + 4, left):
                    stat_tiles(i, k + 4)
                dve.wait_ge(exped, i * (UN // 2) + k // 2 + 1)
                step.done(V.tensor_reduce(n, e3, AX, ALU.add))
                if there(k + 4, left):
                    stat_features(i, k + 4)
                step.wait()
                step.done(V.reciprocal(n, n))
                if hots:
                    one_hot(i, k - 1, 0)
                step.wait()
                step.done(V.tensor_tensor(e3, e3, over[1], ALU.mult))
                if hots:
                    one_hot(i, k - 1, 1)
                step.wait()
                for h in range(2):
                    if not (isinstance(i, int) and i * UN + k < RG):
                        dve.wait_ge(main_done, (i * UN + k + h) * GR - (RG - 1) * GR)
                    own = slice(s + h * GR, s + (h + 1) * GR)
                    at4 = e3[:, h * GR:(h + 1) * GR, :].rearrange("p j (h a) -> p j h a", a=1).to_broadcast([128, GR, HEADS, HF])
                    V.tensor_tensor(msg[:, own, :].rearrange("p j (h d) -> p j h d", h=HEADS),
                                    gt[:, own, 0:F].rearrange("p j (h d) -> p j h d", h=HEADS), at4, ALU.mult).then_inc(msg_ready, 1)
                    if hots:
                        one_hot(i, k - 1, 2 + h)

            def turn(i, left=None):
                for k in range(0, groups(left), 2):
                    if there(k + 2, left):
                        attention(i, k + 2, hots=True, left=left)
                    else:
                        for j in range(2 * GR):
                            one_hot(i, k + j // GR, j % GR)

            for k in range(5):
                stat_tiles(0, k)
                stat_features(0, k)
            attention(0, 0)
            turn(0)
            dve.wait_ge(recs_in, 16)
            before = step.n
            with dve.Fori(1, TURNS - 2) as i:
                step.at = i * PER_TURN - PER_TURN
                turn(i)
                assert step.n == before + PER_TURN
            step.at = 0
            step.n = before + PER_TURN * (TURNS - 3)
            for n, left in enumerate(LEFT):
                turn(TURNS - 2 + n, left)

            for h in range(2):
                dve.wait_ge(half_out[h], NT)
            dve.wait_ge(esum_ready, 1)
            step.done(V.memset(neT[:, DW:NPAD], 0.0))
            V.memset(esum[:, DW:NPAD], 0.0).then_inc(esum_ready, 1)
            for q in range(NB):
                V.tensor_scalar(blk(scr, q), blk(yr, q), 0.0, None, ALU.min).then_inc(elu_in, 1)

            def elu(q):
                dve.wait_ge(elu_in, q + 1)
                step(V.scalar_tensor_tensor(blk(yr, q), blk(yr, q), 0.0, blk(xr, q), ALU.max, ALU.add))
                dve.wait_ge(elu_exp, q + 1)
                step(V.scalar_tensor_tensor(blk(yr, q), blk(scr, q), -1.0, blk(yr, q), ALU.add, ALU.add))

            def wide(v, q):
                own = tiles_of(q)
                return v[:, own].rearrange("p (t a) -> p t a", a=1).to_broadcast([TS, own.stop - own.start, F])

            def add_input(lay, q):
                n = min(NT - q * BT, BT)
                dve.wait_ge(blk_ready, NB * (lay - 1) + q + 1)
                ps = acc[0 if lay == 2 else q % 8][0:TS, 0:n * F].rearrange("p (t f) -> p t f", f=F)
                if lay < 3:
                    V.tensor_tensor(blk(yr, q), ps, blk(xr, q), ALU.add).then_inc(blk_used, 1)
                else:
                    V.scalar_tensor_tensor(blk(yr, q), ps, 0.0, blk(xr, q), ALU.max, ALU.add).then_inc(blk_used, 1)

            def center(lay, q):
                if lay:
                    dve.wait_ge(blk_used, NB * (lay - 1) + q + 1)
                mean = st[0:TS, 0, tiles_of(q)]
                step(V.tensor_reduce(mean, blk(yr, q), AX, ALU.add))
                step(V.tensor_scalar(mean, mean, -1.0 / F, None, ALU.mult))
                step(V.tensor_tensor(blk(xr, q), blk(yr, q), wide(st[0:TS, 0, :], q), ALU.add))
                step(V.tensor_tensor(blk(yr, q), blk(xr, q), blk(xr, q), ALU.mult))
                step(V.tensor_reduce(mean, blk(yr, q), AX, ALU.add))
                ins = V.tensor_scalar(mean, mean, 1.0 / F, EPS, ALU.mult, ALU.add)
                if lay != 2 or q == NB - 1:
                    ins.then_inc(root_in, 1)
                else:
                    step.done(ins)

            def normalize(lay, q):
                dve.wait_ge(root_out, ROOTS[lay] + (0 if lay == 2 else q) + 1)
                own = tiles_of(q)
                step(V.reciprocal(st[0:TS, 2, own], st[0:TS, 1, own]))
                V.tensor_tensor(blk(xr, q), blk(xr, q), wide(st[0:TS, 2, :], q), ALU.mult).then_inc(x_ready, 1)

            def low_half(lay, q):
                dve.wait_ge(xh_ready, NB * lay + q + 1)
                dve.wait_ge(x_ready, NB * lay + q + 1)
                V.scalar_tensor_tensor(blk(xl, q), blk(xr, q), XS, blk(xh, q), ALU.mult, ALU.subtract).then_inc(halves_ready, 1)

            for lay in range(4):
                if lay == 2:
                    for q in range(NB):
                        add_input(lay, q)
                        center(lay, q)
                    step.wait()
                    for q in range(NB + 1):
                        if q < NB:
                            normalize(lay, q)
                        if q:
                            low_half(lay, q - 1)
                else:
                    added = 0
                    for q in range(NB + 2):
                        while lay and added < min(NB, 2 * q + 1):
                            add_input(lay, added)
                            added += 1
                        if lay == 0 and q < NB:
                            elu(q)
                        if q < NB:
                            center(lay, q)
                        if 1 <= q <= NB:
                            normalize(lay, q - 1)
                        if q >= 2 and lay < 3:
                            low_half(lay, q - 2)
                if lay == 0:
                    dve.wait_ge(deg_out, 1)
                    step(V.tensor_scalar(rdeg[:, 0:DW], rdeg[:, 0:DW], 1.0, None, ALU.max))
                    step(V.reciprocal(rdeg[:, 0:DW], rdeg[:, 0:DW]))
                if lay == 1:
                    dve.wait_ge(tile_used, NT * 2)
                    for b, (at, n) in enumerate(DB):
                        V.scalar_tensor_tensor(neT[:, at:at + n], acc[b][:, 0:n], 1.0 / (CS * XS), rdeg[:, at:at + n],
                                               ALU.mult, ALU.mult).then_inc(neigh_out, 1)
    return nc


_INS = ['x', 'src', 'dst', 'edge_attr_16', 'edge_attr_6', 'L0_gnn_W', 'L0_gnn_a', 'L1_gnn_W_neigh', 'L1_gnn_b_neigh',
        'L1_gnn_W_self', 'L1_gnn_b_self', 'L2_gnn_Wg', 'L2_gnn_Ws', 'L2_gnn_bg', 'L2_gnn_W1', 'L2_gnn_b1', 'L2_gnn_W2',
        'L2_gnn_b2', 'L2_gnn_W3', 'L2_gnn_b3', 'L3_gnn_W', 'L3_gnn_b', 'L3_gnn_We', 'L3_gnn_be']


def kernel(**inputs):
    import numpy as _np
    import concourse.bacc as _bacc
    from concourse import mybir as _mybir
    from concourse.bass_utils import run_bass_kernel_spmd as _run

    nc = _bacc.Bacc("TRN2", target_bir_lowering=False, num_devices=1)
    arrays, args = {}, []
    for name in _INS:
        a = _np.ascontiguousarray(inputs[name])
        arrays[f"in_{name}"] = a
        args.append(nc.dram_tensor(f"in_{name}", a.shape, _mybir.dt.from_np(a.dtype), kind="ExternalInput").ap())
    args.append(nc.dram_tensor("out", (N, F), FP32, kind="ExternalOutput").ap())
    gnn_stack(nc, *args)
    r = _run(nc, [arrays], core_ids=[0])
    return r.results[0]["out"]
```
